# Optimizing a Trainium2 kernel written in Bass

```python
import numpy as np
import jax
import jax.numpy as jnp

def _softmax(x, axis=-1):
    return jax.nn.softmax(x, axis=axis)

def _gelu(x):
    return jax.nn.gelu(x, approximate=True)

def _silu(x):
    return jax.nn.silu(x)

def _sigmoid(x):
    return jax.nn.sigmoid(x)

def _layernorm(x, axis=-1, eps=1e-05):
    m = jnp.mean(x, axis=axis, keepdims=True)
    v = jnp.var(x, axis=axis, keepdims=True)
    return (x - m) / jnp.sqrt(v + eps)

def _scatter_add(tgt, idx, src, axis=0):
    return tgt.at[idx].add(src)

def _segment_sum(src, seg, n):
    return jax.ops.segment_sum(src, seg, n)
kernel_name = 'mk_dlrm_tower_d1_rec_r8_26dc84'

def setup_inputs(seed: int=0):
    np.random.seed(seed)
    _w = jnp.asarray

    def _rec_inputs():
        import jax
        import jax.numpy as jnp
        _tk = jax.random.key(seed)
        dense_ctx = jax.random.normal(jax.random.fold_in(_tk, 190), (512, 16), jnp.float32)
        ids = jnp.stack([jax.random.randint(jax.random.fold_in(_tk, 200 + f), (512,), 0, v, jnp.int32) for f, v in enumerate([125000, 1250, 12500, 125000, 125000, 12500, 12500, 125000, 12500, 125000, 12500, 125000, 125000, 1250, 1000, 1250, 12500, 12500, 1250, 1250, 1000, 1000, 1000, 1250, 1250, 1250])], axis=1)
        tbl_0 = 0.05 * jax.random.normal(jax.random.fold_in(_tk, 500 + 0), (125000, 32), jnp.float32)
        tbl_1 = 0.05 * jax.random.normal(jax.random.fold_in(_tk, 500 + 1), (1250, 32), jnp.float32)
        tbl_2 = 0.05 * jax.random.normal(jax.random.fold_in(_tk, 500 + 2), (12500, 32), jnp.float32)
        tbl_3 = 0.05 * jax.random.normal(jax.random.fold_in(_tk, 500 + 3), (125000, 32), jnp.float32)
        tbl_4 = 0.05 * jax.random.normal(jax.random.fold_in(_tk, 500 + 4), (125000, 32), jnp.float32)
        tbl_5 = 0.05 * jax.random.normal(jax.random.fold_in(_tk, 500 + 5), (12500, 32), jnp.float32)
        tbl_6 = 0.05 * jax.random.normal(jax.random.fold_in(_tk, 500 + 6), (12500, 32), jnp.float32)
        tbl_7 = 0.05 * jax.random.normal(jax.random.fold_in(_tk, 500 + 7), (125000, 32), jnp.float32)
        tbl_8 = 0.05 * jax.random.normal(jax.random.fold_in(_tk, 500 + 8), (12500, 32), jnp.float32)
        tbl_9 = 0.05 * jax.random.normal(jax.random.fold_in(_tk, 500 + 9), (125000, 32), jnp.float32)
        tbl_10 = 0.05 * jax.random.normal(jax.random.fold_in(_tk, 500 + 10), (12500, 32), jnp.float32)
        tbl_11 = 0.05 * jax.random.normal(jax.random.fold_in(_tk, 500 + 11), (125000, 32), jnp.float32)
        tbl_12 = 0.05 * jax.random.normal(jax.random.fold_in(_tk, 500 + 12), (125000, 32), jnp.float32)
        tbl_13 = 0.05 * jax.random.normal(jax.random.fold_in(_tk, 500 + 13), (1250, 32), jnp.float32)
        tbl_14 = 0.05 * jax.random.normal(jax.random.fold_in(_tk, 500 + 14), (1000, 32), jnp.float32)
        tbl_15 = 0.05 * jax.random.normal(jax.random.fold_in(_tk, 500 + 15), (1250, 32), jnp.float32)
        tbl_16 = 0.05 * jax.random.normal(jax.random.fold_in(_tk, 500 + 16), (12500, 32), jnp.float32)
        tbl_17 = 0.05 * jax.random.normal(jax.random.fold_in(_tk, 500 + 17), (12500, 32), jnp.float32)
        tbl_18 = 0.05 * jax.random.normal(jax.random.fold_in(_tk, 500 + 18), (1250, 32), jnp.float32)
        tbl_19 = 0.05 * jax.random.normal(jax.random.fold_in(_tk, 500 + 19), (1250, 32), jnp.float32)
        tbl_20 = 0.05 * jax.random.normal(jax.random.fold_in(_tk, 500 + 20), (1000, 32), jnp.float32)
        tbl_21 = 0.05 * jax.random.normal(jax.random.fold_in(_tk, 500 + 21), (1000, 32), jnp.float32)
        tbl_22 = 0.05 * jax.random.normal(jax.random.fold_in(_tk, 500 + 22), (1000, 32), jnp.float32)
        tbl_23 = 0.05 * jax.random.normal(jax.random.fold_in(_tk, 500 + 23), (1250, 32), jnp.float32)
        tbl_24 = 0.05 * jax.random.normal(jax.random.fold_in(_tk, 500 + 24), (1250, 32), jnp.float32)
        tbl_25 = 0.05 * jax.random.normal(jax.random.fold_in(_tk, 500 + 25), (1250, 32), jnp.float32)
        _rk = jax.random.fold_in(_tk, 7)
        W_top1 = 0.0606339 * jax.random.normal(jax.random.fold_in(_tk, 801), (272, 512), jnp.float32)
        W_top2 = 0.0441942 * jax.random.normal(jax.random.fold_in(_tk, 802), (512, 256), jnp.float32)
        W_top3 = 0.0625 * jax.random.normal(jax.random.fold_in(_tk, 803), (256, 1), jnp.float32)
        b_top1 = jnp.zeros((512,), jnp.float32)
        b_top2 = jnp.zeros((256,), jnp.float32)
        return (dense_ctx, ids, tbl_0, tbl_1, tbl_2, tbl_3, tbl_4, tbl_5, tbl_6, tbl_7, tbl_8, tbl_9, tbl_10, tbl_11, tbl_12, tbl_13, tbl_14, tbl_15, tbl_16, tbl_17, tbl_18, tbl_19, tbl_20, tbl_21, tbl_22, tbl_23, tbl_24, tbl_25, W_top1, b_top1, W_top2, b_top2, W_top3)
    dense_ctx, ids, tbl_0, tbl_1, tbl_2, tbl_3, tbl_4, tbl_5, tbl_6, tbl_7, tbl_8, tbl_9, tbl_10, tbl_11, tbl_12, tbl_13, tbl_14, tbl_15, tbl_16, tbl_17, tbl_18, tbl_19, tbl_20, tbl_21, tbl_22, tbl_23, tbl_24, tbl_25, W_top1, b_top1, W_top2, b_top2, W_top3 = _rec_inputs()

    def _L0_rec_setup():
        import jax, jax.numpy as jnp
        import numpy as np
        M_FIELDS = 26
        H1 = 128
        H2 = 128
        BATCH = 256
        EMB_K = 32

        def _cin_layer(x_prev, x0, W, b):
            return jnp.einsum('bik,bjk,hij->bhk', x_prev, x0, W) + b[None, :, None]
        key = jax.random.key(seed)
        k0, k1, k2, k3, k4 = jax.random.split(key, 5)
        inputs = jax.random.normal(k0, (BATCH, M_FIELDS, EMB_K), dtype=jnp.float32)
        W1 = jax.random.normal(k1, (H1, M_FIELDS, M_FIELDS), dtype=jnp.float32) * 0.05
        b1 = jax.random.normal(k2, (H1,), dtype=jnp.float32) * 0.05
        W2 = jax.random.normal(k3, (H2, H1, M_FIELDS), dtype=jnp.float32) * 0.05
        b2 = jax.random.normal(k4, (H2,), dtype=jnp.float32) * 0.05
        return {'inputs': inputs, 'W1': W1, 'b1': b1, 'W2': W2, 'b2': b2}
    _L0_rec_all = _L0_rec_setup()
    _L0_rec_in = {k: v for k, v in _L0_rec_all.items() if k in ('W1', 'b1', 'W2', 'b2')}
    del _L0_rec_all
    return {'dense_ctx': dense_ctx, 'ids': ids, 'tbl_0': tbl_0, 'tbl_1': tbl_1, 'tbl_2': tbl_2, 'tbl_3': tbl_3, 'tbl_4': tbl_4, 'tbl_5': tbl_5, 'tbl_6': tbl_6, 'tbl_7': tbl_7, 'tbl_8': tbl_8, 'tbl_9': tbl_9, 'tbl_10': tbl_10, 'tbl_11': tbl_11, 'tbl_12': tbl_12, 'tbl_13': tbl_13, 'tbl_14': tbl_14, 'tbl_15': tbl_15, 'tbl_16': tbl_16, 'tbl_17': tbl_17, 'tbl_18': tbl_18, 'tbl_19': tbl_19, 'tbl_20': tbl_20, 'tbl_21': tbl_21, 'tbl_22': tbl_22, 'tbl_23': tbl_23, 'tbl_24': tbl_24, 'tbl_25': tbl_25, 'W_top1': W_top1, 'b_top1': b_top1, 'W_top2': W_top2, 'b_top2': b_top2, 'W_top3': W_top3, 'L0_rec_W1': _L0_rec_in['W1'], 'L0_rec_b1': _L0_rec_in['b1'], 'L0_rec_W2': _L0_rec_in['W2'], 'L0_rec_b2': _L0_rec_in['b2']}

def reference(dense_ctx, ids, tbl_0, tbl_1, tbl_2, tbl_3, tbl_4, tbl_5, tbl_6, tbl_7, tbl_8, tbl_9, tbl_10, tbl_11, tbl_12, tbl_13, tbl_14, tbl_15, tbl_16, tbl_17, tbl_18, tbl_19, tbl_20, tbl_21, tbl_22, tbl_23, tbl_24, tbl_25, W_top1, b_top1, W_top2, b_top2, W_top3, L0_rec_W1, L0_rec_b1, L0_rec_W2, L0_rec_b2):
    import jax
    import jax.numpy as jnp

    def _L0_rec_ref(inputs, W1, b1, W2, b2):
        import jax, jax.numpy as jnp
        import numpy as np
        M_FIELDS = 26
        H1 = 128
        H2 = 128
        BATCH = 256
        EMB_K = 32

        def _cin_layer(x_prev, x0, W, b):
            return jnp.einsum('bik,bjk,hij->bhk', x_prev, x0, W) + b[None, :, None]
        x1 = _cin_layer(inputs, inputs, W1, b1)
        x2 = _cin_layer(x1, inputs, W2, b2)
        res = jnp.concatenate([x1, x2], axis=1)
        return jnp.sum(res, axis=-1)
    e = jnp.stack([tbl_0[ids[:, 0]], tbl_1[ids[:, 1]], tbl_2[ids[:, 2]], tbl_3[ids[:, 3]], tbl_4[ids[:, 4]], tbl_5[ids[:, 5]], tbl_6[ids[:, 6]], tbl_7[ids[:, 7]], tbl_8[ids[:, 8]], tbl_9[ids[:, 9]], tbl_10[ids[:, 10]], tbl_11[ids[:, 11]], tbl_12[ids[:, 12]], tbl_13[ids[:, 13]], tbl_14[ids[:, 14]], tbl_15[ids[:, 15]], tbl_16[ids[:, 16]], tbl_17[ids[:, 17]], tbl_18[ids[:, 18]], tbl_19[ids[:, 19]], tbl_20[ids[:, 20]], tbl_21[ids[:, 21]], tbl_22[ids[:, 22]], tbl_23[ids[:, 23]], tbl_24[ids[:, 24]], tbl_25[ids[:, 25]]], axis=1)
    z = _L0_rec_ref(e, L0_rec_W1, L0_rec_b1, L0_rec_W2, L0_rec_b2)
    z = z.reshape(z.shape[0], -1)
    h = jnp.concatenate([z, dense_ctx], axis=1)
    h = jnp.maximum(h @ W_top1 + b_top1, 0.0)
    h = jnp.maximum(h @ W_top2 + b_top2, 0.0)
    y = h @ W_top3
    return y

_drawn_inputs = setup_inputs


def setup_inputs(seed=0):
    import zlib

    import numpy as np

    out = dict(_drawn_inputs(seed))
    spreads = {'b_top1': (0.0, 2.0), 'b_top2': (0.0, 0.8)}
    factors = {'tbl_0': 8.0,
     'tbl_1': 8.0,
     'tbl_2': 8.0,
     'tbl_3': 8.0,
     'tbl_4': 8.0,
     'tbl_5': 8.0,
     'tbl_6': 8.0,
     'tbl_7': 8.0,
     'tbl_8': 8.0,
     'tbl_9': 8.0,
     'tbl_10': 8.0,
     'tbl_11': 8.0,
     'tbl_12': 8.0,
     'tbl_13': 8.0,
     'tbl_14': 8.0,
     'tbl_15': 8.0,
     'tbl_16': 8.0,
     'tbl_17': 8.0,
     'tbl_18': 8.0,
     'tbl_19': 8.0,
     'tbl_20': 8.0,
     'tbl_21': 7.594,
     'tbl_22': 8.0,
     'tbl_23': 8.0,
     'tbl_24': 8.0,
     'tbl_25': 8.0,
     'L0_rec_W1': 8.0,
     'L0_rec_W2': 4.303,
     'dense_ctx': 6.586}
    for name, (base, spread) in spreads.items():
        noise = np.random.default_rng([zlib.crc32(name.encode()), seed]).standard_normal(out[name].shape)
        drawn = base * np.exp(spread * noise) if base else spread * noise
        out[name] = jnp.asarray(drawn.astype(out[name].dtype))
    for name, factor in factors.items():
        out[name] = (out[name] * factor).astype(out[name].dtype)
    return out
```

```python
import concourse.bass as bass
from concourse import mybir
from contextlib import ExitStack

B, F, K, H = 512, 26, 32, 128
P = 128
TILES = B // P
Q = P // K
CH = P // Q
NA, NB, NC = 15, 12, 4
ONE = F
NF = F + 1
DA, DB = NA // 2 + 1, NB // 2
PA = NA * DA
PB = NB * DB + NB // 2
RB = PB + NC * NB
PAIRS = PA + PB + NA * NB
CROSS = PA + PB
JB = NC - 1
CB = NF - JB
XA, XB = NC, NB - 1
NXA = NA - NC
WRAP_A, WRAP_B = DA - 1, DB - 1
EW = WRAP_A + NF + WRAP_B
D_IN, M1, M2 = 16, 512, 256
GC, EG = 8, 4
NG, NE = CH // GC, CH // EG
BANK = 512
FREE = 1


def pair_columns():
    a = [(x, (x + s - WRAP_A) % NA) for s in range(DA) for x in range(NA)]
    b = [(NA + y, NA + (y + d) % NB) for d in range(DB) for y in range(NB)]
    b += [(NA + y, NA + y + DB) for y in range(NB // 2)]
    return a + b + [(x, NA + y) for x in range(NA) for y in range(NB)]


def one_row(b):
    return [set(p) for p in pair_columns()[PA:PA + PB]].index({NA + b, ONE})


def build(nc, ids, tables, w1_xy, w1_yx, w2, b2, dense, wt1, bt1, wt2, bt2, wt3, ident_in, out):
    fp32, i32 = mybir.dt.float32, mybir.dt.int32
    ALU, ACT = mybir.AluOpType, mybir.ActivationFunctionType
    ctx = ExitStack()
    with ctx:
        def sb(name, shape, dt=fp32):
            return ctx.enter_context(nc.sbuf_tensor(name, shape, dt))

        def sem(name):
            return ctx.enter_context(nc.semaphore(name))

        idx = sb("idx", [P, TILES, F], i32)
        rows = sb("rows", [P, F, K])
        ex = sb("ex", [P, CH, EW])
        bd = sb("bd", [P, CH, Q, NF])
        prod = sb("prod", [P, NG, GC, PA + RB])
        TA = sb("TA", [PA, NF, P])
        TB = sb("TB", [RB, CB, P])
        gram = sb("gram", [NXA * XB, P])
        w1a = sb("w1a", [H, PAIRS])
        w1b = sb("w1b", [H, PAIRS])
        w1s = sb("w1s", [H, PAIRS])
        w1x = sb("w1x", [H, NXA * XB])
        w2s = sb("w2s", [H, F, H])
        Fw = sb("Fw", [H, NF, PAIRS])
        wA = sb("wA", [PA, F, H])
        wB = sb("wB", [RB, NF - NC, H])
        v1 = sb("v1", [P, 3, H])
        ident = sb("identity", [P, P])
        b2s = sb("b2s", [H, 1])
        den = sb("den", [D_IN, B])
        t1 = sb("t1", [P, 3, M1])
        t2 = sb("t2", [P, M1 // P, M2])
        t3 = sb("t3", [P, M2 // P])
        c1 = sb("c1", [P, M1 // P])
        c2 = sb("c2", [P, M2 // P])
        Z = sb("Z", [P, 2, P])
        h1 = sb("h1", [P, M1 // P, P])
        h2 = sb("h2", [P, M2 // P, P])
        Y = sb("Y", [1, B])
        ps = [ctx.enter_context(nc.psum_tensor(f"ps{i}", [P, BANK], fp32)) for i in range(8)]
        psA, psB = ps[0:2], ps[2:4]
        psZ = ps[5], ps[4]
        psH1, psH2 = ps[6:8]
        psY = psH2[0:1, M2:M2 + P]

        ids_in, pairs_in, w2_in, top_in = sem("ids_in"), sem("pairs_in"), sem("w2_in"), sem("top_in")
        a_rows, b_rows = sem("a_rows_gathered"), sem("b_rows_gathered")
        a_taken, b_taken = sem("a_rows_transposed"), sem("b_rows_transposed")
        cleared, ones_set = sem("cleared"), sem("ones_set")
        w1_sum, w1_ready = sem("w1_summed"), sem("w1_ready")
        f_done = sem("f_in_psum")
        f_kept = [sem("even_f_in_sbuf"), sem("odd_f_in_sbuf")]
        fold_step, w_folded = sem("fold_step"), sem("weights_folded")
        tr_done, tr_kept = sem("transposed_in_psum"), sem("transposed_in_sbuf")
        v_done, v_kept = sem("z1_weights_in_psum"), sem("z1_weights_in_sbuf")
        ex_step, bd_ready, prod_ready = sem("ex_step"), sem("bd_ready"), sem("prod_ready")
        mom_done, mom_kept = sem("moments_in_psum"), sem("moments_in_sbuf")
        gram_in = sem("gram_in")
        z_done, z_kept = sem("z_in_psum"), sem("z_in_sbuf")
        h1_done, h1_kept = sem("h1_in_psum"), sem("h1_in_sbuf")
        h2_done, h2_kept = sem("h2_in_psum"), sem("h2_in_sbuf")
        y_done, y_kept = sem("y_in_psum"), sem("y_in_sbuf")
        out_done = sem("out_written")

        NFE = F // 2
        NTR = (F + NF - NC + 3) // 4
        slots = [("A", j) for j in range(F)] + [("B", j) for j in range(NC, NF)]
        block = ctx.enter_context(nc.Block())

        @block.sync
        def _(sp):
            sp.dma_start(idx[:], ids.rearrange("(t p) f -> p t f", p=P)).then_inc(ids_in, 16)
            sp.dma_start(w1a[:], w1_xy).then_inc(pairs_in, 16)
            sp.dma_start(w1b[:], w1_yx).then_inc(pairs_in, 16)
            sp.dma_start(w2s[:, 0:NFE, :], w2[:, 0:NFE, :]).then_inc(w2_in, 16)
            sp.dma_start(w2s[:, NFE:F, :], w2[:, NFE:F, :]).then_inc(w2_in, 16)
            sp.dma_start(b2s[:], b2).then_inc(top_in, 16)
            sp.dma_start(ident[:], ident_in).then_inc(top_in, 16)
            sp.dma_start(den[:], dense).then_inc(top_in, 16)
            sp.dma_start(t1[:, 0:2, :], wt1[0:2 * P, :].rearrange("(s p) n -> p s n", p=P)).then_inc(top_in, 16)
            sp.dma_start(t1[0:D_IN, 2, :], wt1[2 * P:2 * P + D_IN, :]).then_inc(top_in, 16)
            sp.dma_start(t2[:], wt2.rearrange("(s p) n -> p s n", p=P)).then_inc(top_in, 16)
            sp.dma_start(t3[:], wt3).then_inc(top_in, 16)
            sp.dma_start(c1[:], bt1).then_inc(top_in, 16)
            sp.dma_start(c2[:], bt2).then_inc(top_in, 16)
            with sp.Fori(FREE + NE, FREE + NE * TILES + 1, NE) as count:
                sp.wait_ge(mom_kept, count)
                sp.wait_ge(z_kept, count)
                for b in range(XB):
                    r = one_row(b)
                    sp.dma_start(gram[b * NXA:(b + 1) * NXA, :],
                                 TB[r:r + 1, XA - JB:XA - JB + NXA, :]).then_inc(gram_in, 16)
            sp.wait_ge(y_kept, TILES)
            sp.dma_start(out, Y[:]).then_inc(out_done, 16)
            sp.wait_ge(out_done, 16)

        @block.gpsimd
        def _(pool):
            pool.wait_ge(ids_in, 16)
            for t in range(TILES):
                for f in range(F):
                    if t > 0 and f == 0:
                        pool.wait_ge(a_taken, t)
                    if t > 0 and f == NA:
                        pool.wait_ge(b_taken, t)
                    nc.gpsimd.indirect_dma_start(
                        rows[:, f, :], None, tables[f],
                        bass.IndirectOffsetOnAxis(ap=idx[:, t, f:f + 1], axis=0),
                    ).then_inc(a_rows if f < NA else b_rows, 16)

        @block.vector
        def _(dve):
            nc.vector.memset(bd[:], 0.0).then_inc(cleared, 1)
            nc.vector.memset(ex[:, :, WRAP_A + ONE:WRAP_A + NF], 1.0).then_inc(ones_set, 1)
            nc.vector.memset(Fw[:, F:NF, :], 0.0)
            dve.wait_ge(cleared, 1)
            for q in range(Q):
                nc.vector.memset(bd[q * K:(q + 1) * K, :, q, ONE:NF], 1.0).then_inc(ones_set, 1)
            dve.wait_ge(pairs_in, 32)
            nc.vector.tensor_tensor(w1s[:], w1a[:], w1b[:], ALU.add).then_inc(w1_sum, 1)
            dve.wait_ge(w1_sum, 1)
            same = WRAP_A * NA
            nc.vector.tensor_copy(w1s[:, same:same + NA + NB], w1a[:, same:same + NA + NB]).then_inc(w1_ready, 1)
            nc.vector.tensor_copy(
                w1x[:].rearrange("h (b a) -> h b a", a=NXA),
                w1s[:, CROSS + NC * NB:PAIRS].rearrange("h (a b) -> h b a", b=NB)[:, 0:XB, :]).then_inc(w1_ready, 1)
            for j in range(1, F, 2):
                dve.wait_ge(f_done, j + 1)
                nc.vector.tensor_copy(Fw[:, j, :], ps[j % 8][:, 0:PAIRS]).then_inc(f_kept[j % 2], 1)

            Fa = lambda j, c, n: Fw[:, j, c:c + n]
            dve.wait_ge(f_kept[0], NFE)
            dve.wait_ge(f_kept[1], NFE)
            dve.wait_ge(top_in, 9 * 16)

            def cross(j0, j1, dj, a0, a1, b0, b1):
                return Fw[:, j0:j1:dj, CROSS:PAIRS].rearrange("h j (a b) -> h j a b", b=NB)[:, :, a0:a1, b0:b1]

            def diagonal(n, j, dj, a, da, b, db, outer, n_outer):
                base = Fw[:, j:j + 1, CROSS + a * NB + b:CROSS + a * NB + b + 1]
                return base, dj * PAIRS + da * NB + db, outer, n_outer, n

            def view(start, steps):
                ap = Fw[:, :, :].rearrange("h j p -> h (j p)")[:, start:start + 1]
                return bass.AP(ap.tensor, ap.offset, [list(ap.ap[0])] + [[s, n] for s, n in steps])

            def add(dst, src, last=False):
                i = nc.vector.tensor_tensor(dst, dst, src, ALU.add)
                if last:
                    i.then_inc(fold_step, 1)

            def runs(shift, n, total):
                cut = [x for x in range(n) if (x + shift) % total == 0 and x > 0]
                edges = [0] + cut + [n]
                return [(x0, (x0 + shift) % total, x1 - x0) for x0, x1 in zip(edges, edges[1:])]

            for order in range(2):
                for s in range(DA):
                    if order and s == WRAP_A:
                        continue
                    for x, y, n in runs(s - WRAP_A, NA, NA):
                        j, a = (x, y) if order == 0 else (y, x)
                        add(view(NA * PAIRS + s * NA + x, [(PAIRS, NB), (1, n)]),
                            view(j * PAIRS + CROSS + a * NB, [(1, NB), (PAIRS + NB, n)]))
                for d in range(DB + 1):
                    if order and d == 0:
                        continue
                    for x, y, n in runs(d, NB if d < DB else NB // 2, NB):
                        j, b = (y, x) if order == 0 else (x, y)
                        add(view(NC * PAIRS + PA + d * NB + x, [(PAIRS, NXA), (1, n)]),
                            view((NA + j) * PAIRS + CROSS + NC * NB + b, [(NB, NXA), (PAIRS + 1, n)]),
                            last=order == 1 and d == DB)
                if order == 0:
                    for d in range(DB + 1):
                        for x, y, n in runs(d, NB if d < DB else NB // 2, NB):
                            add(view((NA + y) * PAIRS + CROSS + x, [(NB, NC), (PAIRS + 1, n)]),
                                view(PA + d * NB + x, [(PAIRS, NC), (1, n)]))
                    i = nc.vector.tensor_copy(Fw[:, F, PA + NB - 1:PA + NB], b2s[:])
                    i.then_inc(fold_step, 1)
                    dve.wait_ge(fold_step, 1)
            dve.wait_ge(fold_step, 2)
            nc.vector.memset(Fw[:, NC:NA, CROSS:CROSS + NC * NB], 0.0).then_inc(w_folded, 1)

            with dve.Fori(0, TILES) as t:
                dve.wait_ge(a_rows, 16 * NA * t + 16 * NA)
                nc.vector.transpose(ex[:, :, WRAP_A:WRAP_A + NA].rearrange("p c f -> p f c"),
                                    rows[:, 0:NA, :]).then_inc(a_taken, 1)
                dve.wait_ge(b_rows, 16 * (F - NA) * t + 16 * (F - NA))
                nc.vector.transpose(ex[:, :, WRAP_A + NA:WRAP_A + F].rearrange("p c f -> p f c"),
                                    rows[:, NA:F, :]).then_inc(b_taken, 1)
                dve.wait_ge(a_taken, t + 1)
                dve.wait_ge(b_taken, t + 1)
                nc.vector.tensor_copy(ex[:, :, 0:WRAP_A], ex[:, :, NA:NA + WRAP_A])
                nc.vector.tensor_copy(ex[:, :, WRAP_A + NF:EW],
                                      ex[:, :, WRAP_A + NA:WRAP_A + NA + WRAP_B]).then_inc(ex_step, 1)
                dve.wait_ge(mom_done, NE * t + FREE)
                for q in range(Q):
                    part = slice(q * K, (q + 1) * K)
                    nc.vector.tensor_copy(bd[part, :, q, 0:F],
                                          ex[part, :, WRAP_A:WRAP_A + F]).then_inc(bd_ready, 1)
                dve.wait_ge(ex_step, t + 1)
                for g in range(NG):
                    c = slice(g * GC, (g + 1) * GC)
                    e = lambda start, steps: bass.AP(ex[:].tensor, ex[:, g * GC, start].offset,
                                                     [list(ex[:].ap[0]), [EW, GC]] + [list(s) for s in steps])
                    o = prod[:, g]
                    nc.vector.tensor_tensor(
                        o[:, :, 0:PA].rearrange("p c (d a) -> p c d a", a=NA),
                        e(WRAP_A, [(0, DA), (1, NA)]), e(0, [(1, DA), (1, NA)]), ALU.mult)
                    nc.vector.tensor_tensor(
                        o[:, :, PA:PA + DB * NB].rearrange("p c (d b) -> p c d b", b=NB),
                        e(WRAP_A + NA, [(0, DB), (1, NB)]), e(WRAP_A + NA, [(1, DB), (1, NB)]), ALU.mult)
                    nc.vector.tensor_tensor(
                        o[:, :, PA + DB * NB:PA + PB], ex[:, c, WRAP_A + NA:WRAP_A + NA + NB // 2],
                        ex[:, c, WRAP_A + NA + DB:WRAP_A + NA + NB], ALU.mult)
                    nc.vector.tensor_tensor(
                        o[:, :, PA + PB:PA + RB].rearrange("p c (a b) -> p c a b", b=NB),
                        e(WRAP_A, [(1, NC), (0, NB)]), e(WRAP_A + NA, [(0, NC), (1, NB)]),
                        ALU.mult).then_inc(prod_ready, 1)
                dve.wait_ge(bd_ready, Q * t + Q)
                dve.wait_ge(prod_ready, NG * t + NG)

        @block.scalar
        def _(act):
            for j in range(0, F, 2):
                act.wait_ge(f_done, j + 1)
                nc.scalar.copy(Fw[:, j, :], ps[j % 8][:, 0:PAIRS]).then_inc(f_kept[j % 2], 1)
            for n in range(NTR):
                act.wait_ge(tr_done, n + 1)
                part = slots[4 * n:4 * n + 4]
                na = sum(k == "A" for k, _ in part)
                src = ps[4 + n % 4][:].rearrange("p (s h) -> p s h", h=H)
                if na:
                    i = nc.scalar.copy(wA[:, part[0][1]:part[0][1] + na, :], src[0:PA, 0:na, :])
                if na < len(part):
                    i = nc.scalar.copy(wB[:, part[na][1] - NC:part[-1][1] - NC + 1, :], src[0:RB, na:len(part), :])
                i.then_inc(tr_kept, 1)
            act.wait_ge(v_done, 1)
            for s, n in enumerate((PA, RB, NXA * XB)):
                i = nc.scalar.copy(v1[0:n, s, :], ps[3][0:n, s * H:(s + 1) * H])
                i.then_inc((mom_kept, z_kept, v_kept)[s], (FREE, FREE + NE, 1)[s])
            act.wait_ge(top_in, 9 * 16)
            with act.Fori(0, TILES) as t:
                for k in range(NE):
                    act.wait_ge(mom_done, NE * t + (k + 1 + FREE))
                    for src, cols, dst, n in ((psA[k % 2], NF, TA, PA), (psB[k % 2], CB, TB, RB)):
                        i = nc.scalar.copy(
                            dst[:].rearrange("p j (q c) -> p c q j", q=Q)[:, k * EG:(k + 1) * EG],
                            src[0:n, 0:EG * Q * cols].rearrange("p (c q j) -> p c q j", c=EG, q=Q))
                    i.then_inc(mom_kept, 1)
                for s in range(2):
                    act.wait_ge(z_done, 2 * t + (s + 1))
                    nc.scalar.copy(Z[:, 1 - s, :], psZ[1 - s][:, 0:P]).then_inc(z_kept, NE // 2)
                act.wait_ge(h1_done, t + 1)
                for m in range(M1 // P):
                    i = nc.scalar.activation(h1[:, m, :], psH1[:, m * P:(m + 1) * P], ACT.Relu, bias=c1[:, m:m + 1])
                i.then_inc(h1_kept, 1)
                act.wait_ge(h2_done, t + 1)
                for m in range(M2 // P):
                    i = nc.scalar.activation(h2[:, m, :], psH2[:, m * P:(m + 1) * P], ACT.Relu, bias=c2[:, m:m + 1])
                i.then_inc(h2_kept, 1)
                act.wait_ge(y_done, t + 1)
                nc.scalar.copy(Y[:, bass.ds(t * P, P)], psY).then_inc(y_kept, 1)

        @block.tensor
        def _(pe):
            pe.wait_ge(w1_ready, 1)
            for j in range(F):
                if j == 0:
                    pe.wait_ge(w2_in, 32)
                if j >= 8:
                    pe.wait_ge(f_kept[j % 2], (j - 8) // 2 + 1)
                nc.tensor.matmul(ps[j % 8][:, 0:PAIRS], w2s[:, j, :], w1s[:],
                                 start=True, stop=True).then_inc(f_done, 1)
            pe.wait_ge(top_in, 9 * 16)
            pe.wait_ge(w1_ready, 2)
            pe.wait_ge(f_kept[0], NFE)
            pe.wait_ge(f_kept[1], NFE)
            nc.tensor.transpose(ps[3][0:PA, 0:H], w1s[:, 0:PA],
                                ident[:]).then_inc(mom_done, FREE)
            nc.tensor.transpose(ps[3][0:RB, H:2 * H], w1s[:, PA:PA + RB], ident[:])
            nc.tensor.transpose(ps[3][0:NXA * XB, 2 * H:3 * H], w1x[:], ident[:]).then_inc(v_done, 1)
            pe.wait_ge(w_folded, 1)
            for n in range(NTR):
                if n >= 4:
                    pe.wait_ge(tr_kept, n - 3)
                for s, (kind, j) in enumerate(slots[4 * n:4 * n + 4]):
                    c, m = (0, PA) if kind == "A" else (PA, RB)
                    i = nc.tensor.transpose(ps[4 + n % 4][0:m, s * H:(s + 1) * H], Fw[:, j, c:c + m], ident[:])
                i.then_inc(tr_done, 1)
            pe.wait_ge(v_kept, 1)
            pe.wait_ge(ones_set, 1 + Q)
            with pe.Fori(0, TILES) as t:
                pe.wait_ge(bd_ready, Q * t + Q)
                for k in range(NE):
                    if k * EG % GC == 0:
                        pe.wait_ge(prod_ready, NG * t + (k * EG // GC + 1))
                    pe.wait_ge(mom_kept, NE * t + (FREE + max(0, k - 1)))
                    for e in range(EG):
                        c = k * EG + e
                        w = prod[:, c // GC, c % GC, :]
                        nc.tensor.matmul(psA[k % 2][0:PA, e * Q * NF:(e + 1) * Q * NF], w[:, 0:PA],
                                         bd[:, c, :, :], start=True, stop=True)
                        i = nc.tensor.matmul(psB[k % 2][0:RB, e * Q * CB:(e + 1) * Q * CB], w[:, PA:PA + RB],
                                             bd[:, c, :, JB:NF], start=True, stop=True)
                    i.then_inc(mom_done, 1)
                pe.wait_ge(mom_kept, NE * t + (FREE + NE))
                pe.wait_ge(z_kept, NE * t + (FREE + NE))
                for n, (kind, j) in enumerate(slots):
                    w, x = (wA[:, j, :], TA[:, j, :]) if kind == "A" else (wB[:, j - NC, :], TB[:, j - JB, :])
                    i = nc.tensor.matmul(psZ[1][:, 0:P], w, x, start=(n == 0), stop=(n == len(slots) - 1))
                i.then_inc(z_done, 1)
                nc.tensor.matmul(psZ[0][:, 0:P], v1[0:PA, 0, :], TA[:, ONE, :], start=True, stop=False)
                nc.tensor.matmul(psZ[0][:, 0:P], v1[0:RB, 1, :], TB[:, ONE - JB, :], start=False, stop=False)
                pe.wait_ge(gram_in, 16 * XB * t + 16 * XB)
                nc.tensor.matmul(psZ[0][:, 0:P], v1[0:NXA * XB, 2, :], gram[:], start=False,
                                 stop=True).then_inc(z_done, 1)
                pe.wait_ge(z_kept, NE * t + (FREE + 2 * NE))
                for m in range(M1 // P):
                    o, cols = psH1[:, m * P:(m + 1) * P], slice(m * P, (m + 1) * P)
                    nc.tensor.matmul(o, t1[:, 1, cols], Z[:, 1, :], start=True, stop=False)
                    nc.tensor.matmul(o, t1[:, 0, cols], Z[:, 0, :], start=False, stop=False)
                    i = nc.tensor.matmul(o, t1[0:D_IN, 2, cols], den[:, bass.ds(t * P, P)], start=False, stop=True)
                i.then_inc(h1_done, 1)
                pe.wait_ge(h1_kept, t + 1)
                for m in range(M2 // P):
                    for s in range(M1 // P):
                        i = nc.tensor.matmul(psH2[:, m * P:(m + 1) * P], t2[:, s, m * P:(m + 1) * P], h1[:, s, :],
                                             start=(s == 0), stop=(s == M1 // P - 1))
                i.then_inc(h2_done, 1)
                pe.wait_ge(h2_kept, t + 1)
                for s in range(M2 // P):
                    i = nc.tensor.matmul(psY, t3[:, s:s + 1], h2[:, s, :],
                                         start=(s == 0), stop=(s == M2 // P - 1))
                i.then_inc(y_done, 1)


def kernel(**inputs):
    import numpy as np
    import concourse.bacc as bacc
    from concourse.bass_utils import run_bass_kernel_spmd

    a = {k: np.asarray(v) for k, v in inputs.items()}
    w1, b1 = a["L0_rec_W1"], a["L0_rec_b1"]
    padded = np.zeros((H, NF, NF), w1.dtype)
    padded[:, :F, :F] = w1
    padded[:, F, F] = b1
    x, y = np.array(pair_columns()).T
    arrays = {
        "ids": np.ascontiguousarray(a["ids"]),
        "w1_xy": np.ascontiguousarray(padded[:, x, y]),
        "w1_yx": np.ascontiguousarray(padded[:, y, x]),
        "w2": np.ascontiguousarray(a["L0_rec_W2"].transpose(1, 2, 0)),
        "b2": np.ascontiguousarray(a["L0_rec_b2"].reshape(H, 1)),
        "dense": np.ascontiguousarray(a["dense_ctx"].T),
        "wt1": np.ascontiguousarray(a["W_top1"]),
        "bt1": np.ascontiguousarray(a["b_top1"].reshape(M1 // P, P).T),
        "wt2": np.ascontiguousarray(a["W_top2"]),
        "bt2": np.ascontiguousarray(a["b_top2"].reshape(M2 // P, P).T),
        "wt3": np.ascontiguousarray(a["W_top3"].reshape(M2 // P, P).T),
        "ident": np.eye(P, dtype=np.float32),
    }
    for f in range(F):
        arrays[f"tbl_{f}"] = np.ascontiguousarray(a[f"tbl_{f}"])
    nc = bacc.Bacc("TRN2", target_bir_lowering=False, num_devices=1)
    ap = {n: nc.dram_tensor(n, v.shape, mybir.dt.from_np(v.dtype), kind="ExternalInput").ap() for n, v in arrays.items()}
    out = nc.dram_tensor("y", (1, B), mybir.dt.float32, kind="ExternalOutput").ap()
    build(nc, ap["ids"], [ap[f"tbl_{f}"] for f in range(F)], ap["w1_xy"], ap["w1_yx"], ap["w2"], ap["b2"],
          ap["dense"], ap["wt1"], ap["bt1"], ap["wt2"], ap["bt2"], ap["wt3"], ap["ident"], out)
    r = run_bass_kernel_spmd(nc, [arrays], core_ids=[0])
    return r.results[0]["y"].reshape(B, 1)
```

```python
import concourse.bass as bass
from concourse import mybir
from contextlib import ExitStack

B, F, K, H = 512, 26, 32, 128
P = 128
TILES = B // P
Q = P // K
CH = P // Q
NA, NB = 14, 12
HA, HB = NA // 2, NB // 2
ONE = F
NF = F + 1
WA, WB = 3, 2
SA, SB = WA + 1, WB + 1
QA, QB = HA * SA, HB * SB + HB // 2
IA, IB = 2 * QA, 2 * QB
PA = IA + HA * HA
PBO = IB + 1 + HB * HB
RB = PBO + NB
CROSS = PA + PBO
PAIRS = CROSS + NB * NA
PK = 64
XA, XB = HA + WA, HB + WB
EB = 2 * XA
EW = EB + 2 * XB
COL_ONE, COL_B = NA, NA + 1
GB = NB // 2
D_IN, M1, M2 = 16, 512, 256
EG = 4
NE = CH // EG
PARTS = ((0, 8), (8, 24))
BY_ACT = 2
BD_B = 2 * Q - BY_ACT
L1_AT = 2
BANK = 512


def pair_columns():
    half_a = [(x, (x + s - WA) % HA) for s in range(SA) for x in range(HA)]
    half_b = [(x, (x + s) % HB) for s in range(SB) for x in range(HB)] + [(x, x + SB) for x in range(HB // 2)]
    shifted = lambda pairs, f: [(x + f, y + f) for x, y in pairs]
    across = lambda f, n: [(f + x, f + n + y) for x in range(n) for y in range(n)]
    a = half_a + shifted(half_a, HA) + across(0, HA)
    b = shifted(half_b, NA) + shifted(half_b, NA + HB) + [(ONE, ONE)] + across(NA, HB)
    return a + b + [(a, NA + b) for b in range(NB) for a in range(NA)]


def build(nc, ids, tables, w1_xy, w1_yx, w2, b2, dense, wt1, bt1, wt2, bt2, wt3, ident_in, out):
    fp32, i32 = mybir.dt.float32, mybir.dt.int32
    ALU, ACT = mybir.AluOpType, mybir.ActivationFunctionType
    ctx = ExitStack()
    with ctx:
        def sb(name, shape, dt=fp32):
            return ctx.enter_context(nc.sbuf_tensor(name, shape, dt))

        def sem(name):
            return ctx.enter_context(nc.semaphore(name))

        idx = sb("idx", [P, TILES, F], i32)
        rows = sb("rows", [P, F, K])
        ex = sb("ex", [P, CH, EW])
        bd = sb("bd", [P, CH, Q, NF])
        prod = sb("prod", [P, CH, PA + RB])
        TA = sb("TA", [PA, 1 + NB, P])
        TB = sb("TB", [RB, NA + 1, P])
        PTA = sb("PTA", [PK + IA, HA, P])
        PTB = sb("PTB", [PK + IB + 1, HB, P])
        gram = sb("gram", [GB * NA, 2, P])
        w1a = sb("w1a", [H, PAIRS])
        w1b = sb("w1b", [H, PAIRS])
        w1s = sb("w1s", [H, PAIRS])
        w2s = sb("w2s", [H, F, H])
        Fw = sb("Fw", [H, F, CROSS])
        Fa = sb("Fa", [H, 2 * XA, NB, 2 * XA])
        Fb = sb("Fb", [H, 2 * XB, 2 * XB, NA])
        Fa1 = sb("Fa1", [H, XA, XA, HA])
        Fa2 = sb("Fa2", [H, XA, HA, XA])
        Fb1 = sb("Fb1", [H, XB, XB, HB])
        Fb2 = sb("Fb2", [H, XB, HB, XB])
        wA = sb("wA", [PA, NB, H])
        wB = sb("wB", [PBO, NA, H])
        wPA = sb("wPA", [PK + IA, HA, H])
        wPB = sb("wPB", [PK + IB + 1, HB, H])
        v1 = sb("v1", [P, 4, H])
        ident = sb("identity", [P, P])
        b2s = sb("b2s", [H, 1])
        b2k = sb("b2k", [H, 1])
        den = sb("den", [D_IN, B])
        t1 = sb("t1", [P, 3, M1])
        t2 = sb("t2", [P, M1 // P, M2])
        t3 = sb("t3", [P, M2 // P])
        c1 = sb("c1", [P, M1 // P])
        c2 = sb("c2", [P, M2 // P])
        Z = sb("Z", [P, 2, P])
        hd = sb("hd", [P, M1 // P, B])
        h1 = sb("h1", [P, M1 // P, P])
        h2 = sb("h2", [P, M2 // P, P])
        Y = sb("Y", [1, B])
        scrap = sb("scrap", [1, 1])
        ps = [ctx.enter_context(nc.psum_tensor(f"ps{i}", [P, BANK], fp32)) for i in range(8)]
        psA, psB = ps[0:2], ps[2:4]
        psZ = ps[5], ps[4]
        psH1, psH2 = ps[6:8]
        psY = psH2[0:1, M2:M2 + P]
        psV = ps[3]

        ids_in, pairs_in, ident_in_sb = sem("ids_in"), sem("pairs_in"), sem("identity_in")
        W2_CUTS = ((NA, NA + 4), (NA + 4, F), (0, NA // 2), (NA // 2, NA))
        w2_in = [sem(f"w2_part{n}_in") for n in range(len(W2_CUTS))]
        top_in = sem("top_in")
        a_rows, b_rows = sem("a_rows_gathered"), [sem("b1_rows_gathered"), sem("b2_rows_gathered")]
        a_taken, b_taken = sem("a_rows_transposed"), [sem("b1_rows_transposed"), sem("b2_rows_transposed")]
        b2_in, b2_ready = sem("b2_in"), sem("b2_ready")
        cleared, ones_set, gap_set = sem("cleared"), sem("ones_set"), sem("gaps_set")
        w1_sum, w1_ready = sem("w1_summed"), sem("w1_ready")
        f_done = sem("f_in_psum")
        f_kept = [sem("f_in_sbuf_by_act"), sem("f_in_sbuf_by_dve")]
        tr_done = sem("transposed_in_psum")
        tr_kept = [sem("transposed_in_sbuf_by_act"), sem("transposed_in_sbuf_by_dve")]
        v_done, v_kept = sem("z1_weights_in_psum"), sem("z1_weights_in_sbuf")
        a_wrapped, b_wrapped = sem("a_fields_repeated"), sem("b_fields_repeated")
        bd_a, bd_b = sem("a_fields_in_block_diagonal"), sem("b_fields_in_block_diagonal_by_dve")
        bd_act = sem("b2_fields_in_block_diagonal_by_act")
        a_prods, b1_prods, b_prods = sem("a_products_ready"), sem("b1_products_ready"), sem("b_products_ready")
        hd_done, hd_kept, h1_sum = sem("dense_part_in_psum"), sem("dense_part_in_sbuf"), sem("h1_summed")
        a_mom_done, b_mom_done = sem("a_moments_in_psum"), sem("b_moments_in_psum")
        a_mom_kept, b_mom_kept = sem("a_moments_in_sbuf"), sem("b_moments_in_sbuf")
        a1_a2_copies, fold_copies, fold_step = sem("a1_a2_copies"), sem("fold_copies"), sem("fold_step")
        inner_folded, w_folded = sem("inner_weights_folded"), sem("mixed_weights_folded")
        gram_in = sem("gram_in")
        z_done, z_kept = sem("z_in_psum"), sem("z_in_sbuf")
        h1_done, h1_kept = sem("h1_in_psum"), sem("h1_in_sbuf")
        h1_kept_act = sem("last_h1_in_sbuf_by_act")
        h2_done, h2_kept = sem("h2_in_psum"), sem("h2_in_sbuf")
        y_done, y_kept = sem("y_in_psum"), sem("y_in_sbuf")
        out_done = sem("out_written")

        by_dve = [n % 2 == 1 and n < 14 for n in range(F)]
        taken = lambda n: sum(d == by_dve[n] for d in by_dve[:n + 1])
        f_order = list(range(NA, F)) + list(range(NA))
        def in_banks(slots):
            return [slots[i:i + 4] for i in range(0, len(slots), 4)]

        early = in_banks([("PB", j) for j in range(NA, F)]) + in_banks([("PA", j) for j in range(NA)])
        late = in_banks([("A", j) for j in range(NA, F)]) + in_banks([("B", j) for j in range(NA)])
        banks = early + late
        weights_by_dve = [n >= len(early) and (n - len(early)) % 2 == 1 for n in range(len(banks))]
        weights_taken = lambda n: sum(d == weights_by_dve[n] for d in weights_by_dve[:n + 1])
        block = ctx.enter_context(nc.Block())

        def view(tensor, start, steps):
            base = tensor[:]
            return bass.AP(base.tensor, base.offset + start, [list(base.ap[0])] + ([[s, n] for s, n in steps if n > 1] or [[1, 1]]))

        def diagonal_a(copy, q):
            part = slice(q * K, (q + 1) * K)
            src = ex[part, :, 0:2 * XA].rearrange("p c (u f) -> p c u f", u=2)[:, :, :, WA:]
            return copy(bd[part, :, q, 0:NA].rearrange("p c (u f) -> p c u f", u=2), src)

        def diagonal_b(copy, q, u):
            part, e0, col = slice(q * K, (q + 1) * K), EB + u * XB, COL_B + u * HB
            return copy(bd[part, :, q, col:col + HB], ex[part, :, e0:e0 + HB])

        def take_f(copy, n):
            j, bank = f_order[n], ps[n % 8]
            copy(Fw[:, j, :], bank[:, 0:CROSS])
            if j < NA:
                mixed = bank[:, CROSS:PAIRS].rearrange("h (b u a) -> h b u a", b=NB, u=2)
                to = Fa[:, j // HA * XA + WA + j % HA].rearrange("h b (u a) -> h b u a", u=2)
                copy(to[:, :, :, 0:WA], mixed[:, :, :, HA - WA:])
                return copy(to[:, :, :, WA:], mixed)
            j -= NA
            mixed = bank[:, CROSS:PAIRS].rearrange("h (u b a) -> h u b a", u=2, a=NA)
            to = Fb[:, j // HB * XB + j % HB].rearrange("h (u b) a -> h u b a", u=2)
            copy(to[:, :, HB:, :], mixed[:, :, 0:WB, :])
            return copy(to[:, :, 0:HB, :], mixed)

        def take_moments(copy, kind, k):
            def put(dst, rows, start, n, col):
                src = (psA if kind == "A" else psB)[k % 2][0:rows, 0:EG * Q * NF]
                return copy(dst[start:start + rows].rearrange("p j (q c) -> p c q j", q=Q)[:, k * EG:(k + 1) * EG],
                            src.rearrange("p (c q j) -> p c q j", c=EG, q=Q)[:, :, :, col:col + n])
            if kind == "A":
                put(TA, PA, 0, 1 + NB, COL_ONE)
                put(PTA, IA, 0, HA, 0)
                return put(PTA, IA, PK, HA, HA)
            put(TB, RB, 0, NA + 1, 0)
            put(PTB, IB + 1, 0, HB, COL_B)
            return put(PTB, IB + 1, PK, HB, COL_B + HB)

        def take_weights(copy, n):
            src = ps[4 + n % 4][:].rearrange("p (s h) -> p s h", h=H)
            runs = []
            for s, (kind, j) in enumerate(banks[n]):
                if kind == "A":
                    place = (wA, 0, PA, j - NA)
                elif kind == "B":
                    place = (wB, 0, PBO, j)
                elif kind == "PA":
                    place = (wPA, j // HA * PK, IA, j % HA)
                else:
                    place = (wPB, (j - NA) // HB * PK, IB + 1, (j - NA) % HB)
                if runs and runs[-1][1][:3] == place[:3]:
                    runs[-1][2] += 1
                else:
                    runs.append([s, place, 1])
            for s, (dst, start, rows, at), count in runs:
                i = copy(dst[start:start + rows, at:at + count, :], src[0:rows, s:s + count, :])
            return i

        @block.sync
        def _(sp):
            sp.dma_start(idx[:], ids.rearrange("(t p) f -> p t f", p=P)).then_inc(ids_in, 16)
            for n, (lo, hi) in enumerate(W2_CUTS):
                sp.dma_start(w2s[:, lo:hi, :], w2[:, lo:hi, :]).then_inc(w2_in[n], 16)
            sp.dma_start(t1[:, 0:2, :], wt1[0:2 * P, :].rearrange("(s p) n -> p s n", p=P)).then_inc(top_in, 16)
            sp.dma_start(t1[0:D_IN, 2, :], wt1[2 * P:2 * P + D_IN, :]).then_inc(top_in, 16)
            sp.dma_start(t2[:], wt2.rearrange("(s p) n -> p s n", p=P)).then_inc(top_in, 16)
            sp.dma_start(t3[:], wt3).then_inc(top_in, 16)
            sp.dma_start(c1[:], bt1).then_inc(top_in, 16)
            sp.dma_start(c2[:], bt2).then_inc(top_in, 16)
            sp.dma_start(den[:], dense).then_inc(top_in, 16)
            with sp.Fori(NE, NE * TILES + 1, NE) as count:
                sp.wait_ge(b_mom_kept, count)
                sp.wait_ge(z_kept, count)
                for b in range(NB):
                    sp.dma_start(gram[b % GB * NA:(b % GB + 1) * NA, b // GB, :],
                                 TB[PBO + b:PBO + b + 1, 0:NA, :]).then_inc(gram_in, 16)
            sp.wait_ge(y_kept, TILES)
            sp.dma_start(out, Y[:]).then_inc(out_done, 16)
            sp.wait_ge(out_done, 16)

        @block.gpsimd
        def _(pool):
            for t in (PTA, PTB):
                nc.gpsimd.memset(t[32:PK], 0.0).then_inc(gap_set, 1)
            pool.wait_ge(ids_in, 16)
            for t in range(TILES):
                for f in range(F):
                    if t > 0 and f == 0:
                        pool.wait_ge(a_taken, t)
                    if t > 0 and f >= NA and (f - NA) % HB == 0:
                        pool.wait_ge(b_taken[(f - NA) // HB], t)
                    nc.gpsimd.indirect_dma_start(
                        rows[:, f, :], None, tables[f],
                        bass.IndirectOffsetOnAxis(ap=idx[:, t, f:f + 1], axis=0),
                    ).then_inc(a_rows if f < NA else b_rows[(f - NA) // HB], 16)

        @block.vector
        def _(dve):
            nc.vector.memset(bd[:], 0.0).then_inc(cleared, 1)
            dve.wait_ge(pairs_in, 32)
            nc.vector.tensor_tensor(w1s[:], w1a[:], w1b[:], ALU.add).then_inc(w1_sum, 1)
            dve.wait_ge(w1_sum, 1)
            for c, step, n in ((WA * HA, QA, HA), (PA, QB, HB), (PA + IB, 1, 1)):
                for_both = [(step, 2), (1, n)] if n > 1 else [(1, 1)]
                nc.vector.tensor_copy(view(w1s, c, for_both), view(w1a, c, for_both)).then_inc(w1_ready, 1)
            nc.vector.memset(prod[:, :, PA + IB:PA + IB + 1], 1.0).then_inc(ones_set, 1)
            dve.wait_ge(cleared, 1)
            for q in range(Q):
                nc.vector.memset(bd[q * K:(q + 1) * K, :, q, COL_ONE:COL_ONE + 1], 1.0).then_inc(ones_set, 1)
            for t in (wPA, wPB):
                nc.vector.memset(t[32:PK], 0.0).then_inc(ones_set, 1)
            for n in range(F):
                if by_dve[n]:
                    dve.wait_ge(f_done, n + 1)
                    take_f(nc.vector.tensor_copy, n).then_inc(f_kept[1], 1)
            dve.wait_ge(b2_in, 16)
            nc.vector.tensor_scalar(b2k[:], b2s[:], float(K), None, ALU.mult).then_inc(b2_ready, 1)

            def circle(c0, chunks, col, e0, wrap, shifts, n):
                return nc.vector.tensor_tensor(
                    view(prod, c0 * (PA + RB) + col, [(PA + RB, chunks), (n, shifts), (1, n)]),
                    view(ex, c0 * EW + e0, [(EW, chunks), (0, shifts), (1, n)]),
                    view(ex, c0 * EW + e0 - wrap, [(EW, chunks), (1, shifts), (1, n)]), ALU.mult)

            def across(c0, chunks, col, e0, e1, n):
                return nc.vector.tensor_tensor(
                    view(prod, c0 * (PA + RB) + col, [(PA + RB, chunks), (n, n), (1, n)]),
                    view(ex, c0 * EW + e0, [(EW, chunks), (1, n), (0, n)]),
                    view(ex, c0 * EW + e1, [(EW, chunks), (0, n), (1, n)]), ALU.mult)

            def halves(lo, hi, width):
                first = 0 if width == XA else EB
                return ex[:, :, first:first + 2 * width].rearrange("p c (u f) -> p c u f", u=2)[:, :, :, lo:hi]

            def arrive_a(t):
                dve.wait_ge(a_rows, 16 * NA * t + 16 * NA)
                for u in range(2):
                    i = nc.vector.transpose(ex[:, :, u * XA + WA:(u + 1) * XA].rearrange("p c f -> p f c"),
                                            rows[:, u * HA:(u + 1) * HA, :])
                i.then_inc(a_taken, 1)

            def part_a(t, used):
                dve.wait_ge(a_taken, t + 1)
                nc.vector.tensor_copy(halves(0, WA, XA), halves(HA, XA, XA)).then_inc(a_wrapped, 1)
                if used is not None:
                    dve.wait_ge(b_mom_done, used)
                for q in range(Q):
                    diagonal_a(nc.vector.tensor_copy, q).then_inc(bd_a, 1)
                across(0, CH, IA, WA, XA + WA, HA)
                dve.wait_ge(a_wrapped, t + 1)
                for u in range(2):
                    i = circle(0, CH, u * QA, u * XA + WA, WA, SA, HA)
                i.then_inc(a_prods, 1)

            def arrive_b(u, t):
                e0 = EB + u * XB
                dve.wait_ge(b_rows[u], 16 * HB * t + 16 * HB)
                nc.vector.transpose(ex[:, :, e0:e0 + HB].rearrange("p c f -> p f c"),
                                    rows[:, NA + u * HB:NA + (u + 1) * HB, :]).then_inc(b_taken[u], 1)
                dve.wait_ge(b_taken[u], t + 1)
                nc.vector.tensor_copy(ex[:, :, e0 + HB:e0 + XB], ex[:, :, e0:e0 + WB]).then_inc(b_wrapped, 1)

            def inside_b(u, c0, chunks):
                e0, col, c = EB + u * XB, PA + u * QB, slice(c0, c0 + chunks)
                one = PA + PBO + u * HB
                nc.vector.tensor_copy(prod[:, c, one:one + HB], ex[:, c, e0:e0 + HB])
                nc.vector.tensor_tensor(prod[:, c, col + SB * HB:col + QB], ex[:, c, e0:e0 + SB],
                                        ex[:, c, e0 + SB:e0 + HB], ALU.mult)
                return circle(c0, chunks, col, e0, 0, SB, HB)

            def part_b(t):
                arrive_b(0, t)
                for q in range(Q):
                    diagonal_b(nc.vector.tensor_copy, q, 0).then_inc(bd_b, 1)
                dve.wait_ge(b_wrapped, 2 * t + 1)
                inside_b(0, 0, CH).then_inc(b1_prods, 1)
                arrive_b(1, t)
                for q in range(BY_ACT, Q):
                    diagonal_b(nc.vector.tensor_copy, q, 1).then_inc(bd_b, 1)
                dve.wait_ge(b_wrapped, 2 * t + 2)
                for c0, chunks in PARTS:
                    across(c0, chunks, PA + IB + 1, EB, EB + XB, HB)
                    inside_b(1, c0, chunks).then_inc(b_prods, 1)
                dve.wait_ge(bd_a, Q * t + Q)
                dve.wait_ge(bd_b, BD_B * t + BD_B)
                dve.wait_ge(bd_act, BY_ACT * t + BY_ACT)
                dve.wait_ge(a_prods, t + 1)
                dve.wait_ge(b1_prods, t + 1)
                dve.wait_ge(b_prods, len(PARTS) * t + len(PARTS))

            def first_layer(t):
                dve.wait_ge(h1_done, t + 1)
                nc.vector.tensor_tensor(h1[:], psH1[:].rearrange("p (m n) -> p m n", n=P),
                                        hd[:, :, bass.ds(t * P, P)], ALU.add).then_inc(h1_sum, 1)
                dve.wait_ge(h1_sum, t + 1)
                nc.vector.tensor_scalar(h1[:], h1[:], 0.0, None, ALU.max).then_inc(h1_kept, 1)

            def add(to, steps, source, start, source_steps):
                dst = view(Fw, to, steps)
                return nc.vector.tensor_tensor(dst, dst, view(source, start, source_steps), ALU.add)

            def fold_a(base, n_j, source, start, sj, sx, sy, second):
                full = SA - second
                at, shift = (WA * sx, sy) if not second else (WA * sy, sx)
                return add(base, [(CROSS, n_j), (HA, full), (1, HA)],
                           source, start + at, [(sj, n_j), (shift, full), (sx + sy, HA)])

            def fold_b(base, n_j, source, start, sj, sx, sy, second):
                shift = sy if second else sx
                add(base + second * HB, [(CROSS, n_j), (HB, SB - second), (1, HB)],
                    source, start + second * shift, [(sj, n_j), (shift, SB - second), (sx + sy, HB)])
                return add(base + SB * HB, [(CROSS, n_j), (1, HB // 2)],
                           source, start + SB * shift, [(sj, n_j), (sx + sy, HB // 2)])

            by_half = lambda t, n: t[:].rearrange("h (u j) b a -> h u j (b a)", u=2)
            AJ, BJ = NB * 2 * XA, 2 * XB * NA

            def fold_inside_b(second):
                fold_b((NA + HB) * CROSS + PA, HB, Fb1, 0, 1, XB * HB, HB, second)
                return fold_b(NA * CROSS + PA + QB, HB, Fb2, 0, XB, HB * XB, 1, second)

            def fold_inside_a(second):
                fold_a(HA * CROSS, HA, Fa1, 0, 1, XA * HA, HA, second)
                return fold_a(QA, HA, Fa2, 0, XA, HA * XA, 1, second)

            def fold_mixed_a(second):
                for u in range(2):
                    fold_a(NA * CROSS + u * QA, NB, Fa, u * XA * (AJ + 1), 2 * XA, AJ, 1, second)
                first, other = ((1, HA), (AJ, HA)) if second else ((AJ, HA), (1, HA))
                return add(NA * CROSS + IA, [(CROSS, NB), (HA, HA), (1, HA)], Fa,
                           (XA + WA) * AJ + WA if second else WA * AJ + XA + WA, [(2 * XA, NB), first, other])

            def fold_mixed_b(second):
                for u in range(2):
                    fold_b(PA + u * QB, NA, Fb, u * XB * (BJ + NA), 1, BJ, NA, second)
                first, other = ((NA, HB), (BJ, HB)) if second else ((BJ, HB), (NA, HB))
                return add(PA + IB + 1, [(CROSS, NA), (HB, HB), (1, HB)], Fb,
                           XB * BJ if second else XB * NA, [(1, NA), first, other])

            dve.wait_ge(f_kept[0], sum(not d for d in by_dve[:NB]))
            dve.wait_ge(f_kept[1], sum(by_dve[:NB]))
            nc.vector.tensor_copy(by_half(Fb, XB)[:, :, HB:XB], by_half(Fb, XB)[:, :, 0:WB])
            b_across = Fw[:, NA:F, PA + IB + 1:CROSS]
            for u, to in enumerate((Fb1, Fb2)):
                src = b_across[:, u * HB:(u + 1) * HB].rearrange("h j (x y) -> h j x y", y=HB)
                nc.vector.tensor_copy(to[:, 0:HB, 0:HB, 0:HB], src)
                if u == 0:
                    nc.vector.tensor_copy(to[:, 0:HB, HB:XB, :], src[:, :, 0:WB, :])
                else:
                    nc.vector.tensor_copy(to[:, 0:HB, :, HB:XB], src[:, :, :, 0:WB])
                i = nc.vector.tensor_copy(to[:, HB:XB, 0:HB, 0:HB], src[:, 0:WB])
            i.then_inc(fold_copies, 1)
            dve.wait_ge(fold_copies, 1)
            fold_inside_b(0).then_inc(fold_step, 1)
            dve.wait_ge(fold_step, 1)
            fold_inside_b(1).then_inc(inner_folded, 1)

            arrive_a(0)
            part_a(0, None)

            dve.wait_ge(f_kept[0], F - sum(by_dve))
            dve.wait_ge(f_kept[1], sum(by_dve))
            nc.vector.tensor_copy(by_half(Fa, XA)[:, :, 0:WA], by_half(Fa, XA)[:, :, HA:XA]).then_inc(fold_copies, 1)
            fold_mixed_b(0)
            dve.wait_ge(a1_a2_copies, 1)
            fold_inside_a(0).then_inc(fold_step, 1)
            dve.wait_ge(fold_copies, 2)
            dve.wait_ge(fold_step, 2)
            fold_inside_a(1).then_inc(inner_folded, 1)
            fold_mixed_a(0).then_inc(fold_step, 1)

            def take_b_moments(k, count):
                dve.wait_ge(b_mom_done, count)
                take_moments(nc.vector.tensor_copy, "B", k).then_inc(b_mom_kept, 1)

            part_b(0)
            dve.wait_ge(fold_step, 3)
            dve.wait_ge(gap_set, 2)
            for k in range(NE):
                take_b_moments(k, k + 1)
                if k == 0:
                    fold_mixed_a(1)
                if k == 1:
                    fold_mixed_b(1).then_inc(w_folded, 1)
            arrive_a(1)
            for n in range(len(banks)):
                if weights_by_dve[n]:
                    dve.wait_ge(tr_done, n + 1)
                    take_weights(nc.vector.tensor_copy, n).then_inc(tr_kept[1], 1)
            part_a(1, NE)
            part_b(1)
            for k in range(NE):
                take_b_moments(k, NE + k + 1)
                if k == L1_AT + 1:
                    first_layer(0)
            with dve.Fori(2, TILES) as t:
                arrive_a(t)
                part_a(t, NE * t)
                part_b(t)
                for k in range(NE):
                    take_b_moments(k, NE * t + (k + 1))
                    if k == L1_AT + 1:
                        first_layer(t - 1)
            for m in range(M1 // P):
                dve.wait_ge(h1_done, TILES + m)
                nc.vector.tensor_tensor(h1[:, m, :], ps[m][:, 0:P], hd[:, m, B - P:B], ALU.add).then_inc(h1_sum, 1)

        @block.scalar
        def _(act):
            act.dma_start(w1a[:], w1_xy).then_inc(pairs_in, 16)
            act.dma_start(w1b[:], w1_yx).then_inc(pairs_in, 16)
            act.dma_start(ident[:], ident_in).then_inc(ident_in_sb, 16)
            act.dma_start(b2s[:], b2).then_inc(b2_in, 16)
            for n in range(F):
                if not by_dve[n]:
                    act.wait_ge(f_done, n + 1)
                    take_f(nc.scalar.copy, n).then_inc(f_kept[0], 1)
            act.wait_ge(f_kept[1], sum(by_dve))
            act.wait_ge(f_kept[0], F - sum(by_dve))
            for u, to in enumerate((Fa1, Fa2)):
                src = Fw[:, u * HA:(u + 1) * HA, IA:PA].rearrange("h j (x y) -> h j x y", y=HA)
                main = to[:, :, WA:, :] if u == 0 else to[:, :, :, WA:]
                nc.scalar.copy(main[:, WA:], src)
                if u == 0:
                    nc.scalar.copy(to[:, WA:, 0:WA, :], src[:, :, HA - WA:, :])
                else:
                    nc.scalar.copy(to[:, WA:, :, 0:WA], src[:, :, :, HA - WA:])
                i = nc.scalar.copy(main[:, 0:WA], src[:, HA - WA:])
            i.then_inc(a1_a2_copies, 1)
            act.wait_ge(v_done, 1)
            for s, n in enumerate((PA, PBO, GB * NA, GB * NA)):
                i = nc.scalar.copy(v1[0:n, s, :], psV[0:n, s * H:(s + 1) * H])
            i.then_inc(v_kept, 1)
            act.wait_ge(top_in, 7 * 16)
            for m in range(M1 // P):
                act.wait_ge(hd_done, m + 1)
                nc.scalar.activation(hd[:, m, :], ps[4 + m][:], ACT.Identity, bias=c1[:, m:m + 1]).then_inc(hd_kept, 1)

            def take_a_moments(k, count):
                act.wait_ge(a_mom_done, count)
                take_moments(nc.scalar.copy, "A", k).then_inc(a_mom_kept, 1)

            def take_z(s, count):
                act.wait_ge(z_done, count)
                nc.scalar.activation(Z[:, s, :], psZ[s][:, 0:P], ACT.Identity,
                                     bias=b2k[:] if s else 0.0).then_inc(z_kept, NE // 2)

            def take_h2(t):
                act.wait_ge(h2_done, t + 1)
                for m in range(M2 // P):
                    i = nc.scalar.activation(h2[:, m, :], psH2[:, m * P:(m + 1) * P], ACT.Relu, bias=c2[:, m:m + 1])
                i.then_inc(h2_kept, 1)

            def take_y(t):
                act.wait_ge(y_done, t + 1)
                nc.scalar.copy(Y[:, bass.ds(t * P, P)], psY).then_inc(y_kept, 1)

            def take_weights_of(group):
                for n in group:
                    if not weights_by_dve[n]:
                        act.wait_ge(tr_done, n + 1)
                        take_weights(nc.scalar.copy, n).then_inc(tr_kept[0], 1)

            act.wait_ge(ones_set, 1 + Q + 2)
            take_weights_of(range(len(early)))
            act.wait_ge(gap_set, 2)
            act.wait_ge(cleared, 1)
            act.wait_ge(v_kept, 1)
            nc.scalar.copy(scrap[:], v1[0:1, 0, 0:1]).then_inc(z_kept, NE)
            def diagonal_b2(t):
                act.wait_ge(b_taken[1], t + 1)
                for q in range(BY_ACT):
                    diagonal_b(nc.scalar.copy, q, 1).then_inc(bd_act, 1)

            diagonal_b2(0)
            for k in range(NE):
                take_a_moments(k, k + 1)
            take_weights_of(range(len(early), len(banks)))
            act.wait_ge(b2_ready, 1)
            take_z(1, 1)
            diagonal_b2(1)
            take_z(0, 2)
            with act.Fori(0, TILES - 2) as t:
                for k in range(NE):
                    take_a_moments(k, NE * t + (NE + k + 1))
                take_h2(t)
                take_z(1, 2 * t + 3)
                take_y(t)
                diagonal_b2(t + 2)
                take_z(0, 2 * t + 4)
            for k in range(NE):
                take_a_moments(k, NE * (TILES - 1) + k + 1)
            take_h2(TILES - 2)
            take_z(1, 2 * TILES - 1)
            take_y(TILES - 2)
            take_z(0, 2 * TILES)
            for m in range(M1 // P):
                act.wait_ge(h1_sum, TILES + m)
                nc.scalar.activation(h1[:, m, :], h1[:, m, :], ACT.Relu).then_inc(h1_kept_act, 1)
            for m in range(M2 // P):
                act.wait_ge(h2_done, TILES + m)
                nc.scalar.activation(h2[:, m, :], ps[6 + m][:, 0:P], ACT.Relu, bias=c2[:, m:m + 1]).then_inc(h2_kept, 1)
            act.wait_ge(y_done, TILES)
            nc.scalar.copy(Y[:, B - P:B], psZ[1][0:1, 0:P]).then_inc(y_kept, 1)

        @block.tensor
        def _(pe):
            pe.wait_ge(w1_ready, 3)
            for n, j in enumerate(f_order):
                for m, (lo, hi) in enumerate(W2_CUTS):
                    if j == lo:
                        pe.wait_ge(w2_in[m], 16)
                if n >= 8:
                    pe.wait_ge(f_kept[by_dve[n - 8]], taken(n - 8))
                nc.tensor.matmul(ps[n % 8][:, 0:PAIRS], w2s[:, j, :], w1s[:],
                                 start=True, stop=True).then_inc(f_done, 1)
            pe.wait_ge(ident_in_sb, 16)
            pe.wait_ge(f_kept[0], F - sum(by_dve))
            pe.wait_ge(f_kept[1], sum(by_dve))
            for s, (c, n) in enumerate(((0, PA), (PA, PBO), (CROSS, GB * NA), (CROSS + GB * NA, GB * NA))):
                i = nc.tensor.transpose(psV[0:n, s * H:(s + 1) * H], w1s[:, c:c + n], ident[:])
            i.then_inc(v_done, 1)
            pe.wait_ge(top_in, 7 * 16)
            for m in range(M1 // P):
                nc.tensor.matmul(ps[4 + m][:], t1[0:D_IN, 2, m * P:(m + 1) * P], den[:],
                                 start=True, stop=True).then_inc(hd_done, 1)

            def moments(k, tile, reuse):
                if k == 0:
                    pe.wait_ge(bd_a, Q * tile + Q)
                    pe.wait_ge(bd_b, BD_B * tile + BD_B)
                    pe.wait_ge(bd_act, BY_ACT * tile + BY_ACT)
                    pe.wait_ge(a_prods, tile + 1)
                    pe.wait_ge(b1_prods, tile + 1)
                for n, (c0, _) in enumerate(PARTS):
                    if k * EG == c0:
                        pe.wait_ge(b_prods, len(PARTS) * tile + (n + 1))
                for bank, col, n, done, kept in ((psA[k % 2], 0, PA, a_mom_done, a_mom_kept),
                                                 (psB[k % 2], PA, RB, b_mom_done, b_mom_kept)):
                    if reuse is not None:
                        pe.wait_ge(kept, reuse)
                    for e in range(EG):
                        c = k * EG + e
                        i = nc.tensor.matmul(bank[0:n, e * Q * NF:(e + 1) * Q * NF], prod[:, c, col:col + n],
                                             bd[:, c, :, :], start=True, stop=True)
                    i.then_inc(done, 1)

            def z2_layer(t):
                pe.wait_ge(a_mom_kept, NE * t + NE)
                pe.wait_ge(b_mom_kept, NE * t + NE)
                pe.wait_ge(z_kept, NE * t + NE)
                terms = ([(wA[:, j, :], TA[:, 1 + j, :]) for j in range(NB)] +
                         [(wB[:, j, :], TB[0:PBO, j, :]) for j in range(NA)] +
                         [(wPA[:, j, :], PTA[:, j, :]) for j in range(HA)] +
                         [(wPB[:, j, :], PTB[:, j, :]) for j in range(HB)])
                for n, (w, x) in enumerate(terms):
                    i = nc.tensor.matmul(psZ[1][:, 0:P], w, x, start=(n == 0), stop=(n == len(terms) - 1))
                i.then_inc(z_done, 1)

            def z1_layer(t):
                nc.tensor.matmul(psZ[0][:, 0:P], v1[0:PA, 0, :], TA[:, 0, :], start=True, stop=False)
                nc.tensor.matmul(psZ[0][:, 0:P], v1[0:PBO, 1, :], TB[0:PBO, NA, :], start=False, stop=False)
                pe.wait_ge(gram_in, 16 * NB * t + 16 * NB)
                for s in range(2):
                    i = nc.tensor.matmul(psZ[0][:, 0:P], v1[0:GB * NA, 2 + s, :], gram[:, s, :],
                                         start=False, stop=(s == 1))
                i.then_inc(z_done, 1)

            def layer1(t):
                pe.wait_ge(z_kept, NE * t + 2 * NE)
                for m in range(M1 // P):
                    o, cols = psH1[:, m * P:(m + 1) * P], slice(m * P, (m + 1) * P)
                    nc.tensor.matmul(o, t1[:, 1, cols], Z[:, 1, :], start=True, stop=False)
                    i = nc.tensor.matmul(o, t1[:, 0, cols], Z[:, 0, :], start=False, stop=True)
                i.then_inc(h1_done, 1)

            def layer2(t):
                pe.wait_ge(h1_kept, t + 1)
                for m in range(M2 // P):
                    for s in range(M1 // P):
                        i = nc.tensor.matmul(psH2[:, m * P:(m + 1) * P], t2[:, s, m * P:(m + 1) * P], h1[:, s, :],
                                             start=(s == 0), stop=(s == M1 // P - 1))
                i.then_inc(h2_done, 1)

            def layer3(t):
                pe.wait_ge(h2_kept, t + 1)
                for s in range(M2 // P):
                    i = nc.tensor.matmul(psY, t3[:, s:s + 1], h2[:, s, :], start=(s == 0), stop=(s == M2 // P - 1))
                i.then_inc(y_done, 1)

            def transpose_weights(group):
                for n in group:
                    if n < 4:
                        pe.wait_ge(hd_kept, n + 1)
                    else:
                        pe.wait_ge(tr_kept[weights_by_dve[n - 4]], weights_taken(n - 4))
                    for s, (kind, j) in enumerate(banks[n]):
                        c, m = {"A": (0, PA), "B": (PA, PBO), "PA": (0, IA), "PB": (PA, IB + 1)}[kind]
                        i = nc.tensor.transpose(ps[4 + n % 4][0:m, s * H:(s + 1) * H], Fw[:, j, c:c + m], ident[:])
                    i.then_inc(tr_done, 1)

            in_b = len(in_banks(range(NB)))
            pe.wait_ge(inner_folded, 1)
            transpose_weights(range(in_b))
            pe.wait_ge(inner_folded, 2)
            transpose_weights(range(in_b, len(early)))
            pe.wait_ge(v_kept, 1)
            pe.wait_ge(ones_set, 1 + Q + 2)
            for k in range(NE):
                moments(k, 0, k - 1 if k >= 2 else None)
            pe.wait_ge(w_folded, 1)
            transpose_weights(range(len(early), len(banks)))
            for kept, by in ((tr_kept[0], False), (tr_kept[1], True)):
                pe.wait_ge(kept, sum(d == by for d in weights_by_dve))
            z2_layer(0)
            z1_layer(0)
            with pe.Fori(0, TILES - 1) as t:
                for k in range(NE):
                    moments(k, t + 1, NE * t + (NE + max(0, k - 1)))
                    if k == L1_AT:
                        layer1(t)
                layer2(t)
                z2_layer(t + 1)
                layer3(t)
                z1_layer(t + 1)
            last = NE * (TILES - 1)
            for s, kept in ((1, last + NE + NE // 2), (0, last + 2 * NE)):
                pe.wait_ge(z_kept, kept)
                for m in range(M1 // P):
                    i = nc.tensor.matmul(ps[m][:, 0:P], t1[:, s, m * P:(m + 1) * P], Z[:, s, :],
                                         start=(s == 1), stop=(s == 0))
                    if s == 0:
                        i.then_inc(h1_done, 1)
            for s in range(M1 // P):
                pe.wait_ge(h1_kept_act, s + 1)
                for m in range(M2 // P):
                    i = nc.tensor.matmul(ps[6 + m][:, 0:P], t2[:, s, m * P:(m + 1) * P], h1[:, s, :],
                                         start=(s == 0), stop=(s == M1 // P - 1))
                    if s == M1 // P - 1:
                        i.then_inc(h2_done, 1)
            for s in range(M2 // P):
                pe.wait_ge(h2_kept, TILES + s)
                i = nc.tensor.matmul(psZ[1][0:1, 0:P], t3[:, s:s + 1], h2[:, s, :], start=(s == 0), stop=(s == M2 // P - 1))
            i.then_inc(y_done, 1)


def kernel(**inputs):
    import numpy as np
    import concourse.bacc as bacc
    from concourse.bass_utils import run_bass_kernel_spmd

    a = {k: np.asarray(v) for k, v in inputs.items()}
    w1, b1 = a["L0_rec_W1"], a["L0_rec_b1"]
    padded = np.zeros((H, NF, NF), w1.dtype)
    padded[:, :F, :F] = w1
    padded[:, F, F] = b1
    x, y = np.array(pair_columns()).T
    arrays = {
        "ids": np.ascontiguousarray(a["ids"]),
        "w1_xy": np.ascontiguousarray(padded[:, x, y]),
        "w1_yx": np.ascontiguousarray(padded[:, y, x]),
        "w2": np.ascontiguousarray(a["L0_rec_W2"].transpose(1, 2, 0)),
        "b2": np.ascontiguousarray(a["L0_rec_b2"].reshape(H, 1)),
        "dense": np.ascontiguousarray(a["dense_ctx"].T),
        "wt1": np.ascontiguousarray(a["W_top1"]),
        "bt1": np.ascontiguousarray(a["b_top1"].reshape(M1 // P, P).T),
        "wt2": np.ascontiguousarray(a["W_top2"]),
        "bt2": np.ascontiguousarray(a["b_top2"].reshape(M2 // P, P).T),
        "wt3": np.ascontiguousarray(a["W_top3"].reshape(M2 // P, P).T),
        "ident": np.eye(P, dtype=np.float32),
    }
    for f in range(F):
        arrays[f"tbl_{f}"] = np.ascontiguousarray(a[f"tbl_{f}"])
    nc = bacc.Bacc("TRN2", target_bir_lowering=False, num_devices=1)
    ap = {n: nc.dram_tensor(n, v.shape, mybir.dt.from_np(v.dtype), kind="ExternalInput").ap() for n, v in arrays.items()}
    out = nc.dram_tensor("y", (1, B), mybir.dt.float32, kind="ExternalOutput").ap()
    build(nc, ap["ids"], [ap[f"tbl_{f}"] for f in range(F)], ap["w1_xy"], ap["w1_yx"], ap["w2"], ap["b2"],
          ap["dense"], ap["wt1"], ap["bt1"], ap["wt2"], ap["bt2"], ap["wt3"], ap["ident"], out)
    r = run_bass_kernel_spmd(nc, [arrays], core_ids=[0])
    return r.results[0]["y"].reshape(B, 1)
```

```python
import concourse.bass as bass
from concourse import mybir
from contextlib import ExitStack

B, F, K, H = 512, 26, 32, 128
P = 128
TILES = B // P
Q = P // K
CH = P // Q
NA, NB = 14, 12
HA, HB = NA // 2, NB // 2
ONE = F
NF = F + 1
WA, WB = 3, 2
SA, SB = WA + 1, WB + 1
QA, QB = HA * SA, HB * SB + HB // 2
IA, IB = 2 * QA, 2 * QB
PA = IA + HA * HA
PBO = IB + 1 + HB * HB
GUEST = PBO + IB + 1
B_ONE = 96
RB = B_ONE + NB
CROSS = PA + PBO
PAIRS = CROSS + NB * NA
PK = 64
XA, XB = HA + WA, HB + WB
EB = 2 * XA
EW = EB + 2 * XB
COL_ONE, COL_B = NA, NA + 1
GT = 3
GX = NB - GT
V1_COLS = ((0, PA), (PA, PBO + GT * NA), (CROSS + GT * NA, GX * NA))
D_IN, M1, M2 = 16, 512, 256
EG = 4
NE = CH // EG
PARTS = ((0, 4), (4, 12), (16, 16))
LOOKED = (20, 21)
NL, CUTS = len(LOOKED), 3
VP, VS = 125, 8
REST = B - P
BY_ACT = 2
BD_B = 2 * Q - BY_ACT
L1_TAKEN_AT = 1
BANK = 512


def pair_columns():
    half_a = [(x, (x + s - WA) % HA) for s in range(SA) for x in range(HA)]
    half_b = [(x, (x + s) % HB) for s in range(SB) for x in range(HB)] + [(x, x + SB) for x in range(HB // 2)]
    shifted = lambda pairs, f: [(x + f, y + f) for x, y in pairs]
    across = lambda f, n: [(f + x, f + n + y) for x in range(n) for y in range(n)]
    a = half_a + shifted(half_a, HA) + across(0, HA)
    b = shifted(half_b, NA) + shifted(half_b, NA + HB) + [(ONE, ONE)] + across(NA, HB)
    return a + b + [(a, NA + b) for b in range(NB) for a in range(NA)]


def build(nc, ids, tables, ids_looked, row_of, w1_xy, w1_yx, w2, b2, dense, wt1, bt1, wt2, bt2, wt3, ident_in, out):
    fp32, i32, fp16, bf16 = mybir.dt.float32, mybir.dt.int32, mybir.dt.float16, mybir.dt.bfloat16
    ALU, ACT = mybir.AluOpType, mybir.ActivationFunctionType
    ctx = ExitStack()
    with ctx:
        def sb(name, shape, dt=fp32):
            return ctx.enter_context(nc.sbuf_tensor(name, shape, dt))

        def sem(name):
            return ctx.enter_context(nc.semaphore(name))

        idx = sb("idx", [P, TILES, F], i32)
        rows = sb("rows", [P, F, K])
        ex = sb("ex", [P, CH, EW])
        bd = sb("bd", [P, CH, Q, NF])
        prod = sb("prod", [P, CH, PA + RB])
        TA = sb("TA", [PA, 1 + NB, P])
        TB = sb("TB", [GUEST, NA + 1, P])
        PTA = sb("PTA", [PK + IA, HA, P])
        inner = sb("inner", [IB + 1, NB, P])
        b_one = sb("b_one", [NB, NA, P])
        gram = sb("gram", [GX * NA, P])
        w1a = sb("w1a", [H, PAIRS])
        w1b = sb("w1b", [H, PAIRS])
        w1s = sb("w1s", [H, PAIRS])
        w2s = sb("w2s", [H, F, H])
        Fw = sb("Fw", [H, F, CROSS])
        Fa = sb("Fa", [H, 2 * XA, NB, 2 * XA])
        Fb = sb("Fb", [H, 2 * XB, 2 * XB, NA])
        Fa1 = sb("Fa1", [H, XA, XA, HA])
        Fa2 = sb("Fa2", [H, XA, HA, XA])
        Fb1 = sb("Fb1", [H, XB, XB, HB])
        Fb2 = sb("Fb2", [H, XB, HB, XB])
        wPA = sb("wPA", [PK + IA, HA, H])
        w_inner = sb("w_inner", [IB + 1, NB, H])
        v1 = sb("v1", [P, 3, H])
        ident = sb("identity", [P, P])
        lids = sb("looked_ids", [VP, NL, REST], i32)
        lids16 = sb("looked_ids_fp16", [VP, NL, REST], fp16)
        row_no = sb("row_no", [VP, VS])
        tab = sb("tab", [VP, NL, VS, K])
        rest = sb("tab_rest", [VP, NL, VS, K])
        cuts = sb("tab_parts", [VP, NL, VS, CUTS, K], bf16)
        hot = sb("one_hot", [VP, NL, VS, REST], bf16)
        looked = sb("looked", [P, TILES, NL, K])
        b2s = sb("b2s", [H, 1])
        b2k = sb("b2k", [H, 1])
        den = sb("den", [D_IN, B])
        t1 = sb("t1", [P, 3, M1])
        t2 = sb("t2", [P, M1 // P, M2])
        t3 = sb("t3", [P, M2 // P])
        c1 = sb("c1", [P, M1 // P])
        c2 = sb("c2", [P, M2 // P])
        Y = sb("Y", [1, B])

        def in_place_of(tensor, start, shape):
            axes = "abcd"[:len(tensor.shape) - 1]
            flat = tensor[0:shape[0]].rearrange(f"p {' '.join(axes)} -> p ({' '.join(axes)})")
            return flat[:, start:start + shape[1] * shape[2]].rearrange("p (x y) -> p x y", y=shape[2])

        wA = in_place_of(Fa, 0, [PA, NB, H])
        wB = in_place_of(Fa, NB * H, [GUEST, NA, H])
        hd = in_place_of(w2s, 0, [P, M1 // P, B])
        h1 = in_place_of(Fb, 0, [P, M1 // P, P])
        h2 = in_place_of(Fb, M1, [P, M2 // P, P])
        Z = in_place_of(Fb, M1 + M2, [P, 2, P])
        scrap = sb("scrap", [1, 1])
        ps = [ctx.enter_context(nc.psum_tensor(f"ps{i}", [P, BANK], fp32)) for i in range(8)]
        psA, psB = ps[0:2], ps[2:4]
        psZ = ps[5], ps[4]
        psH1, psH2 = ps[6:8]
        psY = psH2[0:1, M2:M2 + P]
        psV = ps[3]
        LW = NL * CUTS * K
        psL = {1: ps[7][:, 0:LW], 2: ps[7][:, LW:2 * LW], 3: ps[5][:, 0:LW]}

        ids_in, pairs_in, ident_in_sb = sem("ids_in"), sem("pairs_in"), sem("identity_in")
        W2_CUTS = ((NA, NA + 4), (NA + 4, F), (0, NA // 2), (NA // 2, NA))
        w2_in = [sem(f"w2_part{n}_in") for n in range(len(W2_CUTS))]
        top_in = sem("top_in")
        lids_in, row_no_in, tab_in = sem("looked_ids_in"), sem("row_numbers_in"), sem("looked_tables_in")
        lids_ready = sem("looked_ids_ready")
        part_cut, rest_left, hot_ready = sem("table_part_cut"), sem("table_rest_left"), sem("one_hot_ready")
        looked_done, looked_kept = sem("looked_up_in_psum"), sem("looked_up_in_sbuf")
        looked_placed = sem("looked_up_rows_placed")
        a_rows, b_rows = sem("a_rows_gathered"), [sem("b1_rows_gathered"), sem("b2_rows_gathered")]
        a_taken, b_taken = sem("a_rows_transposed"), [sem("b1_rows_transposed"), sem("b2_rows_transposed")]
        b2_in, b2_ready = sem("b2_in"), sem("b2_ready")
        cleared, ones_set, gap_set = sem("cleared"), sem("ones_set"), sem("gaps_set")
        w1_sum, w1_ready = sem("w1_summed"), sem("w1_ready")
        f_done = sem("f_in_psum")
        f_kept = [sem("f_in_sbuf_by_act"), sem("f_in_sbuf_by_dve")]
        tr_done = sem("transposed_in_psum")
        tr_kept = sem("transposed_in_sbuf")
        v_done, v_kept = sem("z1_weights_in_psum"), sem("z1_weights_in_sbuf")
        a_wrapped, b_wrapped = sem("a_fields_repeated"), sem("b_fields_repeated")
        bd_a, bd_b = sem("a_fields_in_block_diagonal"), sem("b_fields_in_block_diagonal_by_dve")
        bd_act = sem("b2_fields_in_block_diagonal_by_act")
        a_prods, b1_prods, b_prods = sem("a_products_ready"), sem("b1_products_ready"), sem("b_products_ready")
        hd_done, hd_kept, h1_sum = sem("dense_part_in_psum"), sem("dense_part_in_sbuf"), sem("h1_summed")
        a_mom_done, b_mom_done = sem("a_moments_in_psum"), sem("b_moments_in_psum")
        a_mom_kept, b_mom_kept = sem("a_moments_in_sbuf"), sem("b_moments_in_sbuf")
        a1_a2_copies, fa_wrapped = sem("a1_a2_copies"), sem("fa_j_repeated")
        fold_copies, fold_step = sem("fold_copies"), sem("fold_step")
        inner_folded, mixed_folded = sem("inner_weights_folded"), sem("mixed_weights_folded")
        gram_in, guests_in, w_guests_in = sem("gram_in"), sem("guests_in"), sem("guest_weights_in")
        z_done, z_kept = sem("z_in_psum"), sem("z_in_sbuf")
        h1_done, h1_kept = sem("h1_in_psum"), sem("h1_in_sbuf")
        h1_kept_act = sem("last_h1_in_sbuf_by_act")
        h2_done, h2_kept = sem("h2_in_psum"), sem("h2_in_sbuf")
        y_done, y_kept = sem("y_in_psum"), sem("y_in_sbuf")
        out_done = sem("out_written")

        by_dve = [n % 2 == 1 and n < 14 for n in range(F)]
        taken = lambda n: sum(d == by_dve[n] for d in by_dve[:n + 1])
        f_order = list(range(NA, F)) + list(range(NA))

        def in_banks(slots):
            return [slots[i:i + 4] for i in range(0, len(slots), 4)]

        early = in_banks([("PB", j) for j in range(NA, F)]) + in_banks([("PA", j) for j in range(NA)])
        late = in_banks([("A", j) for j in range(NA, F)]) + in_banks([("B", j) for j in range(NA)])
        banks = early + late
        bank_of = [4 + n % 4 for n in range(len(early))] + [4, 6, 0, 7, 5, 1, 2]
        block = ctx.enter_context(nc.Block())

        def view(tensor, start, steps):
            base = tensor[:]
            free = [[s, n] for s, n in steps if n > 1] or [[1, 1]]
            return bass.AP(base.tensor, base.offset + start, [list(base.ap[0])] + free)

        def diagonal_a(copy, q):
            part = slice(q * K, (q + 1) * K)
            src = ex[part, :, 0:2 * XA].rearrange("p c (u f) -> p c u f", u=2)[:, :, :, WA:]
            return copy(bd[part, :, q, 0:NA].rearrange("p c (u f) -> p c u f", u=2), src)

        def diagonal_b(copy, q, u):
            part, e0, col = slice(q * K, (q + 1) * K), EB + u * XB, COL_B + u * HB
            return copy(bd[part, :, q, col:col + HB], ex[part, :, e0:e0 + HB])

        def take_f(copy, n):
            j, bank = f_order[n], ps[n % 8]
            copy(Fw[:, j, :], bank[:, 0:CROSS])
            if j < NA:
                mixed = bank[:, CROSS:PAIRS].rearrange("h (b u a) -> h b u a", b=NB, u=2)
                to = Fa[:, j // HA * XA + WA + j % HA].rearrange("h b (u a) -> h b u a", u=2)
                copy(to[:, :, :, 0:WA], mixed[:, :, :, HA - WA:])
                return copy(to[:, :, :, WA:], mixed)
            j -= NA
            mixed = bank[:, CROSS:PAIRS].rearrange("h (u b a) -> h u b a", u=2, a=NA)
            to = Fb[:, j // HB * XB + j % HB].rearrange("h (u b) a -> h u b a", u=2)
            copy(to[:, :, HB:, :], mixed[:, :, 0:WB, :])
            return copy(to[:, :, 0:HB, :], mixed)

        def take_moments(copy, kind, k):
            def put(dst, rows, start, n, col, row=0):
                src = (psA if kind == "A" else psB)[k % 2][row:row + rows, 0:EG * Q * NF]
                return copy(dst[start:start + rows].rearrange("p j (q c) -> p c q j", q=Q)[:, k * EG:(k + 1) * EG],
                            src.rearrange("p (c q j) -> p c q j", c=EG, q=Q)[:, :, :, col:col + n])
            if kind == "A":
                put(TA, PA, 0, 1 + NB, COL_ONE)
                put(PTA, IA, 0, HA, 0)
                return put(PTA, IA, PK, HA, HA)
            put(inner, IB + 1, 0, NB, COL_B)
            put(TB, PBO, 0, NA + 1, 0)
            return put(b_one, NB, 0, NA, 0, B_ONE)

        def take_weights(copy, n):
            src = ps[bank_of[n]][:].rearrange("p (s h) -> p s h", h=H)
            runs = []
            for s, (kind, j) in enumerate(banks[n]):
                if kind == "A":
                    place = (wA, 0, PA, j - NA)
                elif kind == "B":
                    place = (wB, 0, PBO, j)
                elif kind == "PA":
                    place = (wPA, j // HA * PK, IA, j % HA)
                else:
                    place = (w_inner, 0, IB + 1, j - NA)
                if runs and runs[-1][1][:3] == place[:3]:
                    runs[-1][2] += 1
                else:
                    runs.append([s, place, 1])
            for s, (dst, start, rows, at), count in runs:
                i = copy(dst[start:start + rows, at:at + count, :], src[0:rows, s:s + count, :])
            return i

        by_half = lambda t: t[:].rearrange("h (u j) b a -> h u j (b a)", u=2)

        @block.sync
        def _(sp):
            sp.dma_start(idx[:], ids.rearrange("(t p) f -> p t f", p=P)).then_inc(ids_in, 16)
            for n, (lo, hi) in enumerate(W2_CUTS):
                sp.dma_start(w2s[:, lo:hi, :], w2[:, lo:hi, :]).then_inc(w2_in[n], 16)
                if n == 0:
                    sp.dma_start(lids[:], ids_looked[:, P:B].partition_broadcast(VP)).then_inc(lids_in, 16)
                    sp.dma_start(row_no[:], row_of).then_inc(row_no_in, 16)
            for l, f in enumerate(LOOKED):
                sp.dma_start(tab[:, l], tables[f].rearrange("(p v) k -> p v k", p=VP)).then_inc(tab_in, 16)
            sp.dma_start(t1[:, 0:2, :], wt1[0:2 * P, :].rearrange("(s p) n -> p s n", p=P)).then_inc(top_in, 16)
            sp.dma_start(t1[0:D_IN, 2, :], wt1[2 * P:2 * P + D_IN, :]).then_inc(top_in, 16)
            sp.dma_start(t2[:], wt2.rearrange("(s p) n -> p s n", p=P)).then_inc(top_in, 16)
            sp.dma_start(t3[:], wt3).then_inc(top_in, 16)
            sp.dma_start(c1[:], bt1).then_inc(top_in, 16)
            sp.dma_start(c2[:], bt2).then_inc(top_in, 16)
            sp.dma_start(den[:], dense).then_inc(top_in, 16)
            sp.wait_ge(tr_kept, len(early))
            sp.wait_ge(mixed_folded, 2)
            sp.dma_start(wB[PBO:GUEST, 0:NB, :], w_inner[:]).then_inc(w_guests_in, 16)
            with sp.Fori(NE, NE * TILES + 1, NE) as count:
                sp.wait_ge(b_mom_kept, count)
                sp.wait_ge(z_kept, count)
                sp.dma_start(TB[PBO:GUEST, 0:NB, :], inner[:]).then_inc(guests_in, 16)
                sp.dma_start(TB[PBO:PBO + GT * NA, NA, :], b_one[0:GT]).then_inc(gram_in, 16)
                sp.dma_start(gram[:], b_one[GT:NB]).then_inc(gram_in, 16)
            sp.wait_ge(y_kept, TILES)
            sp.dma_start(out, Y[:]).then_inc(out_done, 16)
            sp.wait_ge(out_done, 16)

        @block.gpsimd
        def _(pool):
            nc.gpsimd.memset(PTA[32:PK], 0.0).then_inc(gap_set, 1)
            pool.wait_ge(ids_in, 16)
            for t in range(TILES):
                for f in range(F):
                    if t > 0 and f in LOOKED:
                        continue
                    if t > 0 and f == 0:
                        pool.wait_ge(a_taken, t)
                    if t > 0 and f in (NA, max(LOOKED) + 1):
                        pool.wait_ge(b_taken[(f - NA) // HB], t)
                    nc.gpsimd.indirect_dma_start(
                        rows[:, f, :], None, tables[f],
                        bass.IndirectOffsetOnAxis(ap=idx[:, t, f:f + 1], axis=0),
                    ).then_inc(a_rows if f < NA else b_rows[(f - NA) // HB], 16)

        @block.vector
        def _(dve):
            nc.vector.memset(bd[:], 0.0).then_inc(cleared, 1)
            dve.wait_ge(pairs_in, 32)
            nc.vector.tensor_tensor(w1s[:], w1a[:], w1b[:], ALU.add).then_inc(w1_sum, 1)
            dve.wait_ge(w1_sum, 1)
            for c, step, n in ((WA * HA, QA, HA), (PA, QB, HB), (PA + IB, 1, 1)):
                for_both = [(step, 2), (1, n)] if n > 1 else [(1, 1)]
                nc.vector.tensor_copy(view(w1s, c, for_both), view(w1a, c, for_both)).then_inc(w1_ready, 1)
            nc.vector.memset(prod[:, :, PA + IB:PA + IB + 1], 1.0).then_inc(ones_set, 1)
            dve.wait_ge(cleared, 1)
            for q in range(Q):
                nc.vector.memset(bd[q * K:(q + 1) * K, :, q, COL_ONE:COL_ONE + 1], 1.0).then_inc(ones_set, 1)
            nc.vector.memset(wPA[32:PK], 0.0).then_inc(ones_set, 1)
            nc.vector.memset(prod[:, :, PA + PBO:PA + B_ONE], 0.0).then_inc(ones_set, 1)

            def one_hot(steps):
                for n in steps:
                    if n == 0:
                        dve.wait_ge(row_no_in, 16)
                        dve.wait_ge(lids_ready, 1)
                    l, v = divmod(n, VS)
                    nc.vector.tensor_scalar(hot[:, l, v, :], lids16[:, l, :], row_no[:, v:v + 1], None,
                                            ALU.is_equal).then_inc(hot_ready, 1)

            def table_rest(n):
                dve.wait_ge(part_cut, n + 1)
                if n > 0:
                    dve.wait_ge(rest_left, n)
                nc.vector.tensor_tensor(rest[:], (rest if n else tab)[:], cuts[:, :, :, n, :],
                                        ALU.subtract).then_inc(rest_left, 1)

            hot_steps = {3: range(0, 6), 5: range(6, 10), 7: range(10, 13), 11: range(13, 16)}
            for n in range(F):
                if by_dve[n]:
                    one_hot(hot_steps.get(n, ()))
                    if n in (9, 13):
                        table_rest(n // 4 - 2)
                    dve.wait_ge(f_done, n + 1)
                    take_f(nc.vector.tensor_copy, n).then_inc(f_kept[1], 1)
            dve.wait_ge(b2_in, 16)
            nc.vector.tensor_scalar(b2k[:], b2s[:], float(K), None, ALU.mult).then_inc(b2_ready, 1)

            def circle(c0, chunks, col, e0, wrap, shifts, n):
                return nc.vector.tensor_tensor(
                    view(prod, c0 * (PA + RB) + col, [(PA + RB, chunks), (n, shifts), (1, n)]),
                    view(ex, c0 * EW + e0, [(EW, chunks), (0, shifts), (1, n)]),
                    view(ex, c0 * EW + e0 - wrap, [(EW, chunks), (1, shifts), (1, n)]), ALU.mult)

            def across(c0, chunks, col, e0, e1, n):
                return nc.vector.tensor_tensor(
                    view(prod, c0 * (PA + RB) + col, [(PA + RB, chunks), (n, n), (1, n)]),
                    view(ex, c0 * EW + e0, [(EW, chunks), (1, n), (0, n)]),
                    view(ex, c0 * EW + e1, [(EW, chunks), (0, n), (1, n)]), ALU.mult)

            def halves_a(lo, hi):
                return ex[:, :, 0:2 * XA].rearrange("p c (u f) -> p c u f", u=2)[:, :, :, lo:hi]

            def arrive_a(t):
                dve.wait_ge(a_rows, 16 * NA * t + 16 * NA)
                for u in range(2):
                    i = nc.vector.transpose(ex[:, :, u * XA + WA:(u + 1) * XA].rearrange("p c f -> p f c"),
                                            rows[:, u * HA:(u + 1) * HA, :])
                i.then_inc(a_taken, 1)

            def part_a(t, used):
                dve.wait_ge(a_taken, t + 1)
                nc.vector.tensor_copy(halves_a(0, WA), halves_a(HA, XA)).then_inc(a_wrapped, 1)
                if used is not None:
                    dve.wait_ge(b_mom_done, used)
                for q in range(Q):
                    diagonal_a(nc.vector.tensor_copy, q).then_inc(bd_a, 1)
                across(0, CH, IA, WA, XA + WA, HA)
                dve.wait_ge(a_wrapped, t + 1)
                for u in range(2):
                    i = circle(0, CH, u * QA, u * XA + WA, WA, SA, HA)
                i.then_inc(a_prods, 1)

            def arrive_b(u, t):
                e0 = EB + u * XB
                gathers = HB - NL if u else HB
                dve.wait_ge(b_rows[u], 16 * gathers * t + 16 * HB)
                nc.vector.transpose(ex[:, :, e0:e0 + HB].rearrange("p c f -> p f c"),
                                    rows[:, NA + u * HB:NA + (u + 1) * HB, :]).then_inc(b_taken[u], 1)
                dve.wait_ge(b_taken[u], t + 1)
                nc.vector.tensor_copy(ex[:, :, e0 + HB:e0 + XB], ex[:, :, e0:e0 + WB]).then_inc(b_wrapped, 1)

            def inside_b(u, c0, chunks):
                e0, col, c = EB + u * XB, PA + u * QB, slice(c0, c0 + chunks)
                one = PA + B_ONE + u * HB
                nc.vector.tensor_copy(prod[:, c, one:one + HB], ex[:, c, e0:e0 + HB])
                nc.vector.tensor_tensor(prod[:, c, col + SB * HB:col + QB], ex[:, c, e0:e0 + SB],
                                        ex[:, c, e0 + SB:e0 + HB], ALU.mult)
                return circle(c0, chunks, col, e0, 0, SB, HB)

            def place_looked(t):
                nc.vector.tensor_copy(rows[:, LOOKED[0]:LOOKED[0] + NL, :].rearrange("p f k -> p (f k)"),
                                      looked[:, bass.ds(t, 1), :, :].rearrange("p t f k -> p (t f k)")
                                      ).then_inc(looked_placed, 1)
                dve.wait_ge(looked_placed, t)

            def part_b1(t):
                arrive_b(0, t)
                for q in range(Q):
                    diagonal_b(nc.vector.tensor_copy, q, 0).then_inc(bd_b, 1)
                dve.wait_ge(b_wrapped, 2 * t + 1)
                inside_b(0, 0, CH).then_inc(b1_prods, 1)

            def part_b2(t):
                arrive_b(1, t)
                for q in range(BY_ACT, Q):
                    diagonal_b(nc.vector.tensor_copy, q, 1).then_inc(bd_b, 1)
                dve.wait_ge(b_wrapped, 2 * t + 2)
                for c0, chunks in PARTS:
                    across(c0, chunks, PA + IB + 1, EB, EB + XB, HB)
                    inside_b(1, c0, chunks).then_inc(b_prods, 1)
                dve.wait_ge(bd_a, Q * t + Q)
                dve.wait_ge(bd_b, BD_B * t + BD_B)
                dve.wait_ge(bd_act, BY_ACT * t + BY_ACT)
                dve.wait_ge(a_prods, t + 1)
                dve.wait_ge(b1_prods, t + 1)
                dve.wait_ge(b_prods, len(PARTS) * t + len(PARTS))

            def first_layer(t):
                dve.wait_ge(h1_done, t + 1)
                nc.vector.tensor_tensor(h1[:], psH1[:].rearrange("p (m n) -> p m n", n=P),
                                        hd[:, :, bass.ds(t * P, P)], ALU.add).then_inc(h1_sum, 1)
                dve.wait_ge(h1_sum, t + 1)
                nc.vector.tensor_scalar(h1[:], h1[:], 0.0, None, ALU.max).then_inc(h1_kept, 1)

            def add(to, steps, source, start, source_steps):
                dst = view(Fw, to, steps)
                return nc.vector.tensor_tensor(dst, dst, view(source, start, source_steps), ALU.add)

            def fold_a(base, n_j, source, start, sj, sx, sy, second):
                full = SA - second
                at, shift = (WA * sx, sy) if not second else (WA * sy, sx)
                return add(base, [(CROSS, n_j), (HA, full), (1, HA)],
                           source, start + at, [(sj, n_j), (shift, full), (sx + sy, HA)])

            def fold_b(base, n_j, source, start, sj, sx, sy, second):
                shift = sy if second else sx
                add(base + second * HB, [(CROSS, n_j), (HB, SB - second), (1, HB)],
                    source, start + second * shift, [(sj, n_j), (shift, SB - second), (sx + sy, HB)])
                return add(base + SB * HB, [(CROSS, n_j), (1, HB // 2)],
                           source, start + SB * shift, [(sj, n_j), (sx + sy, HB // 2)])

            AJ, BJ = NB * 2 * XA, 2 * XB * NA

            def fold_inside_b(second):
                fold_b((NA + HB) * CROSS + PA, HB, Fb1, 0, 1, XB * HB, HB, second)
                return fold_b(NA * CROSS + PA + QB, HB, Fb2, 0, XB, HB * XB, 1, second)

            def fold_inside_a(second):
                fold_a(HA * CROSS, HA, Fa1, 0, 1, XA * HA, HA, second)
                return fold_a(QA, HA, Fa2, 0, XA, HA * XA, 1, second)

            def fold_mixed_a(second, half_pairs):
                if half_pairs:
                    for u in range(2):
                        i = fold_a(NA * CROSS + u * QA, NB, Fa, u * XA * (AJ + 1), 2 * XA, AJ, 1, second)
                    return i
                first, other = ((1, HA), (AJ, HA)) if second else ((AJ, HA), (1, HA))
                return add(NA * CROSS + IA, [(CROSS, NB), (HA, HA), (1, HA)], Fa,
                           (XA + WA) * AJ + WA if second else WA * AJ + XA + WA, [(2 * XA, NB), first, other])

            def fold_mixed_b(second, half_pairs):
                if half_pairs:
                    for u in range(2):
                        i = fold_b(PA + u * QB, NA, Fb, u * XB * (BJ + NA), 1, BJ, NA, second)
                    return i
                first, other = ((NA, HB), (BJ, HB)) if second else ((BJ, HB), (NA, HB))
                return add(PA + IB + 1, [(CROSS, NA), (HB, HB), (1, HB)], Fb,
                           XB * BJ if second else XB * NA, [(1, NA), first, other])

            dve.wait_ge(f_kept[0], sum(not d for d in by_dve[:NB]))
            dve.wait_ge(f_kept[1], sum(by_dve[:NB]))
            nc.vector.tensor_copy(by_half(Fb)[:, :, HB:XB], by_half(Fb)[:, :, 0:WB])
            b_across = Fw[:, NA:F, PA + IB + 1:CROSS]
            for u, to in enumerate((Fb1, Fb2)):
                src = b_across[:, u * HB:(u + 1) * HB].rearrange("h j (x y) -> h j x y", y=HB)
                nc.vector.tensor_copy(to[:, 0:HB, 0:HB, 0:HB], src)
                if u == 0:
                    nc.vector.tensor_copy(to[:, 0:HB, HB:XB, :], src[:, :, 0:WB, :])
                else:
                    nc.vector.tensor_copy(to[:, 0:HB, :, HB:XB], src[:, :, :, 0:WB])
                i = nc.vector.tensor_copy(to[:, HB:XB, 0:HB, 0:HB], src[:, 0:WB])
            i.then_inc(fold_copies, 1)
            dve.wait_ge(fold_copies, 1)
            fold_inside_b(0).then_inc(fold_step, 1)
            dve.wait_ge(fold_step, 1)
            fold_inside_b(1).then_inc(inner_folded, 1)

            arrive_a(0)
            part_a(0, None)

            dve.wait_ge(a1_a2_copies, 1)
            fold_inside_a(0).then_inc(fold_step, 1)
            dve.wait_ge(fold_step, 2)
            fold_inside_a(1).then_inc(inner_folded, 1)

            part_b1(0)
            dve.wait_ge(f_kept[0], F - sum(by_dve))
            dve.wait_ge(f_kept[1], sum(by_dve))
            fold_mixed_a(0, True)
            fold_mixed_a(0, False).then_inc(fold_step, 1)
            part_b2(0)
            dve.wait_ge(looked_done, TILES - 1)
            for t in range(1, TILES):
                nc.vector.tensor_reduce(looked[:, t, :, :], psL[t].rearrange("p (l s k) -> p l k s", l=NL, s=CUTS),
                                        mybir.AxisListType.X, ALU.add).then_inc(looked_kept, 1)
            dve.wait_ge(looked_kept, TILES - 1)

            def take_b_moments(k, count):
                dve.wait_ge(b_mom_done, count)
                take_moments(nc.vector.tensor_copy, "B", k).then_inc(b_mom_kept, 1)

            for k in range(NE):
                take_b_moments(k, k + 1)
                if k == 0:
                    fold_mixed_b(0, True)
                if k == 1:
                    fold_mixed_b(0, False).then_inc(fold_step, 1)
                if k == 2:
                    dve.wait_ge(fa_wrapped, 1)
                    dve.wait_ge(fold_step, 3)
                    fold_mixed_a(1, True)
                if k == 3:
                    fold_mixed_a(1, False).then_inc(mixed_folded, 1)
                if k == 4:
                    dve.wait_ge(fold_step, 4)
                    fold_mixed_b(1, True)
                if k == 5:
                    fold_mixed_b(1, False).then_inc(mixed_folded, 1)
            arrive_a(1)
            part_a(1, NE)
            part_b1(1)
            place_looked(1)
            part_b2(1)
            for k in range(NE):
                take_b_moments(k, NE + k + 1)
                if k == L1_TAKEN_AT:
                    first_layer(0)
            with dve.Fori(2, TILES) as t:
                arrive_a(t)
                part_a(t, NE * t)
                part_b1(t)
                place_looked(t)
                part_b2(t)
                for k in range(NE):
                    take_b_moments(k, NE * t + (k + 1))
                    if k == L1_TAKEN_AT:
                        first_layer(t - 1)
            for m in range(M1 // P):
                dve.wait_ge(h1_done, TILES + m)
                nc.vector.tensor_tensor(h1[:, m, :], ps[m][:, 0:P], hd[:, m, B - P:B], ALU.add).then_inc(h1_sum, 1)

        @block.scalar
        def _(act):
            act.dma_start(w1a[:], w1_xy).then_inc(pairs_in, 16)
            act.dma_start(w1b[:], w1_yx).then_inc(pairs_in, 16)
            act.dma_start(ident[:], ident_in).then_inc(ident_in_sb, 16)
            act.dma_start(b2s[:], b2).then_inc(b2_in, 16)

            def table_part(n):
                if n == 0:
                    act.wait_ge(tab_in, 16 * NL)
                else:
                    act.wait_ge(rest_left, n)
                nc.scalar.copy(cuts[:, :, :, n, :], (rest if n else tab)[:]).then_inc(part_cut, 1)

            for n in range(F):
                if not by_dve[n]:
                    act.wait_ge(f_done, n + 1)
                    take_f(nc.scalar.copy, n).then_inc(f_kept[0], 1)
                if n == 0:
                    act.wait_ge(lids_in, 16)
                    nc.scalar.copy(lids16[:], lids[:]).then_inc(lids_ready, 1)
                if n in (6, 10, 14):
                    table_part(n // 4 - 1)
            act.wait_ge(f_kept[1], sum(by_dve))
            act.wait_ge(f_kept[0], F - sum(by_dve))
            for u, to in enumerate((Fa1, Fa2)):
                src = Fw[:, u * HA:(u + 1) * HA, IA:PA].rearrange("h j (x y) -> h j x y", y=HA)
                main = to[:, :, WA:, :] if u == 0 else to[:, :, :, WA:]
                nc.scalar.copy(main[:, WA:], src)
                if u == 0:
                    nc.scalar.copy(to[:, WA:, 0:WA, :], src[:, :, HA - WA:, :])
                else:
                    nc.scalar.copy(to[:, WA:, :, 0:WA], src[:, :, :, HA - WA:])
                i = nc.scalar.copy(main[:, 0:WA], src[:, HA - WA:])
            i.then_inc(a1_a2_copies, 1)
            act.wait_ge(v_done, 1)
            for s, (_, n) in enumerate(V1_COLS):
                i = nc.scalar.copy(v1[0:n, s, :], psV[0:n, s * H:(s + 1) * H])
            i.then_inc(v_kept, 1)
            act.wait_ge(top_in, 7 * 16)
            for m in range(M1 // P):
                act.wait_ge(hd_done, m + 1)
                nc.scalar.activation(hd[:, m, :], ps[4 + m][:], ACT.Identity, bias=c1[:, m:m + 1]).then_inc(hd_kept, 1)

            def take_a_moments(k, count):
                act.wait_ge(a_mom_done, count)
                take_moments(nc.scalar.copy, "A", k).then_inc(a_mom_kept, 1)

            def take_z(s, count):
                act.wait_ge(z_done, count)
                nc.scalar.activation(Z[:, s, :], psZ[s][:, 0:P], ACT.Identity,
                                     bias=b2k[:] if s else 0.0).then_inc(z_kept, NE // 2)

            def take_h2(t):
                act.wait_ge(h2_done, t + 1)
                for m in range(M2 // P):
                    i = nc.scalar.activation(h2[:, m, :], psH2[:, m * P:(m + 1) * P], ACT.Relu, bias=c2[:, m:m + 1])
                i.then_inc(h2_kept, 1)

            def take_y(t):
                act.wait_ge(y_done, t + 1)
                nc.scalar.copy(Y[:, bass.ds(t * P, P)], psY).then_inc(y_kept, 1)

            def take_weights_of(group):
                for n in group:
                    act.wait_ge(tr_done, n + 1)
                    take_weights(nc.scalar.copy, n).then_inc(tr_kept, 1)

            act.wait_ge(ones_set, 1 + Q + 2)
            take_weights_of(range(len(early)))
            act.wait_ge(gap_set, 1)
            act.wait_ge(cleared, 1)
            act.wait_ge(v_kept, 1)
            nc.scalar.copy(scrap[:], v1[0:1, 0, 0:1]).then_inc(z_kept, NE)

            def diagonal_b2(t):
                act.wait_ge(b_taken[1], t + 1)
                for q in range(BY_ACT):
                    diagonal_b(nc.scalar.copy, q, 1).then_inc(bd_act, 1)

            diagonal_b2(0)
            nc.scalar.copy(by_half(Fa)[:, :, 0:WA], by_half(Fa)[:, :, HA:XA]).then_inc(fa_wrapped, 1)
            for k in range(NE):
                take_a_moments(k, k + 1)
            take_weights_of(range(len(early), len(banks)))
            act.wait_ge(b2_ready, 1)
            take_z(1, 1)
            diagonal_b2(1)
            take_z(0, 2)
            with act.Fori(0, TILES - 2) as t:
                for k in range(NE):
                    take_a_moments(k, NE * t + (NE + k + 1))
                take_h2(t)
                take_z(1, 2 * t + 3)
                take_y(t)
                diagonal_b2(t + 2)
                take_z(0, 2 * t + 4)
            for k in range(NE):
                take_a_moments(k, NE * (TILES - 1) + k + 1)
            take_h2(TILES - 2)
            take_z(1, 2 * TILES - 1)
            take_y(TILES - 2)
            take_z(0, 2 * TILES)
            for m in range(M1 // P):
                act.wait_ge(h1_sum, TILES + m)
                nc.scalar.activation(h1[:, m, :], h1[:, m, :], ACT.Relu).then_inc(h1_kept_act, 1)
            for m in range(M2 // P):
                act.wait_ge(h2_done, TILES + m)
                nc.scalar.activation(h2[:, m, :], ps[6 + m][:, 0:P], ACT.Relu, bias=c2[:, m:m + 1]).then_inc(h2_kept, 1)
            act.wait_ge(y_done, TILES)
            nc.scalar.copy(Y[:, B - P:B], psZ[1][0:1, 0:P]).then_inc(y_kept, 1)

        @block.tensor
        def _(pe):
            pe.wait_ge(w1_ready, 3)
            for n, j in enumerate(f_order):
                for m, (lo, hi) in enumerate(W2_CUTS):
                    if j == lo:
                        pe.wait_ge(w2_in[m], 16)
                if n >= 8:
                    pe.wait_ge(f_kept[by_dve[n - 8]], taken(n - 8))
                nc.tensor.matmul(ps[n % 8][:, 0:PAIRS], w2s[:, j, :], w1s[:],
                                 start=True, stop=True).then_inc(f_done, 1)
            pe.wait_ge(ident_in_sb, 16)
            last_f = F - 8 + 1
            pe.wait_ge(f_kept[by_dve[last_f]], taken(last_f))
            for s, (c, n) in enumerate(V1_COLS):
                i = nc.tensor.transpose(psV[0:n, s * H:(s + 1) * H], w1s[:, c:c + n], ident[:])
            i.then_inc(v_done, 1)
            pe.wait_ge(top_in, 7 * 16)
            for m in range(M1 // P):
                pe.wait_ge(f_kept[by_dve[F - 6 + m]], taken(F - 6 + m))
                nc.tensor.matmul(ps[4 + m][:], t1[0:D_IN, 2, m * P:(m + 1) * P], den[:],
                                 start=True, stop=True).then_inc(hd_done, 1)

            def moments(k, tile, reuse):
                if k == 0:
                    pe.wait_ge(bd_a, Q * tile + Q)
                    pe.wait_ge(bd_b, BD_B * tile + BD_B)
                    pe.wait_ge(bd_act, BY_ACT * tile + BY_ACT)
                    pe.wait_ge(a_prods, tile + 1)
                    pe.wait_ge(b1_prods, tile + 1)
                for n, (c0, _) in enumerate(PARTS):
                    if k * EG == c0:
                        pe.wait_ge(b_prods, len(PARTS) * tile + (n + 1))
                for bank, col, n, done, kept in ((psA[k % 2], 0, PA, a_mom_done, a_mom_kept),
                                                 (psB[k % 2], PA, RB, b_mom_done, b_mom_kept)):
                    if reuse is not None:
                        pe.wait_ge(kept, reuse)
                    for e in range(EG):
                        c = k * EG + e
                        i = nc.tensor.matmul(bank[0:n, e * Q * NF:(e + 1) * Q * NF], prod[:, c, col:col + n],
                                             bd[:, c, :, :], start=True, stop=True)
                    i.then_inc(done, 1)

            def weights_kept(kinds):
                pe.wait_ge(tr_kept, max(n for n, slots in enumerate(banks) if slots[0][0] in kinds) + 1)

            def z2_layer(t, first=False):
                if first:
                    weights_kept(("A",))
                pe.wait_ge(a_mom_kept, NE * t + NE)
                pe.wait_ge(b_mom_kept, NE * t + NE)
                pe.wait_ge(z_kept, NE * t + NE)
                terms = ([(wA[:, j, :], TA[:, 1 + j, :]) for j in range(NB)] +
                         [(wPA[:, j, :], PTA[:, j, :]) for j in range(HA)] +
                         [(wB[0:PBO, j, :], TB[0:PBO, j, :]) for j in range(NB, NA)] +
                         [(wB[:, j, :], TB[:, j, :]) for j in range(NB)])
                for n, (w, x) in enumerate(terms):
                    if first and n == NB + HA:
                        weights_kept(("B",))
                    if n == len(terms) - NB:
                        if first:
                            pe.wait_ge(w_guests_in, 16)
                        pe.wait_ge(guests_in, 16 * t + 16)
                    i = nc.tensor.matmul(psZ[1][:, 0:P], w, x, start=(n == 0), stop=(n == len(terms) - 1))
                i.then_inc(z_done, 1)

            def z1_layer(t):
                nc.tensor.matmul(psZ[0][:, 0:P], v1[0:PA, 0, :], TA[:, 0, :], start=True, stop=False)
                pe.wait_ge(gram_in, 32 * t + 32)
                n = V1_COLS[1][1]
                nc.tensor.matmul(psZ[0][:, 0:P], v1[0:n, 1, :], TB[0:n, NA, :], start=False, stop=False)
                i = nc.tensor.matmul(psZ[0][:, 0:P], v1[0:GX * NA, 2, :], gram[:], start=False, stop=True)
                i.then_inc(z_done, 1)

            def layer1(t):
                for s, kept in ((1, NE + NE // 2), (0, 2 * NE)):
                    pe.wait_ge(z_kept, NE * t + kept)
                    for m in range(M1 // P):
                        i = nc.tensor.matmul(psH1[:, m * P:(m + 1) * P], t1[:, s, m * P:(m + 1) * P], Z[:, s, :],
                                             start=(s == 1 and m == 0), stop=(s == 0 and m == M1 // P - 1))
                i.then_inc(h1_done, 1)

            def layer2(t):
                pe.wait_ge(h1_kept, t + 1)
                for m in range(M2 // P):
                    for s in range(M1 // P):
                        i = nc.tensor.matmul(psH2[:, m * P:(m + 1) * P], t2[:, s, m * P:(m + 1) * P], h1[:, s, :],
                                             start=(s == 0), stop=(s == M1 // P - 1))
                i.then_inc(h2_done, 1)

            def layer3(t):
                pe.wait_ge(h2_kept, t + 1)
                for s in range(M2 // P):
                    i = nc.tensor.matmul(psY, t3[:, s:s + 1], h2[:, s, :], start=(s == 0), stop=(s == M2 // P - 1))
                i.then_inc(y_done, 1)

            def transpose_weights(group):
                for n in group:
                    if n < 4:
                        pe.wait_ge(hd_kept, n + 1)
                    elif n < len(early):
                        pe.wait_ge(tr_kept, n - 3)
                    for s, (kind, j) in enumerate(banks[n]):
                        c, m = {"A": (0, PA), "B": (PA, PBO), "PA": (0, IA), "PB": (PA, IB + 1)}[kind]
                        i = nc.tensor.transpose(ps[bank_of[n]][0:m, s * H:(s + 1) * H], Fw[:, j, c:c + m], ident[:])
                    i.then_inc(tr_done, 1)

            in_b = len(in_banks(range(NB)))
            pe.wait_ge(inner_folded, 1)
            transpose_weights(range(in_b))
            pe.wait_ge(inner_folded, 2)
            transpose_weights(range(in_b, len(early)))
            pe.wait_ge(hot_ready, NL * VS)
            pe.wait_ge(part_cut, CUTS)
            last_in = max(n for n in range(len(early)) if bank_of[n] in (5, 7))
            pe.wait_ge(tr_kept, last_in + 1)
            for t in range(1, TILES):
                for l in range(NL):
                    o = psL[t][:, l * CUTS * K:(l + 1) * CUTS * K]
                    for v in range(VS):
                        i = nc.tensor.matmul(o, hot[:, l, v, (t - 1) * P:t * P],
                                             cuts[:, l, v].rearrange("p s k -> p (s k)"), start=(v == 0), stop=(v == VS - 1))
                i.then_inc(looked_done, 1)
            pe.wait_ge(v_kept, 1)
            pe.wait_ge(ones_set, 1 + Q + 2)
            for k in range(NE):
                moments(k, 0, k - 1 if k >= 2 else None)
            pe.wait_ge(tr_kept, len(early))
            pe.wait_ge(a_mom_kept, NE)
            pe.wait_ge(mixed_folded, 1)
            transpose_weights([n for n, slots in enumerate(banks) if slots[0][0] == "A"])
            pe.wait_ge(looked_kept, TILES - 1)
            pe.wait_ge(b_mom_kept, NE)
            pe.wait_ge(mixed_folded, 2)
            transpose_weights([n for n, slots in enumerate(banks) if slots[0][0] == "B"])
            z2_layer(0, first=True)
            z1_layer(0)
            with pe.Fori(0, TILES - 1) as t:
                layer1(t)
                for k in range(NE):
                    moments(k, t + 1, NE * t + (NE + max(0, k - 1)))
                layer2(t)
                z2_layer(t + 1)
                layer3(t)
                z1_layer(t + 1)
            last = NE * (TILES - 1)
            for s, kept in ((1, last + NE + NE // 2), (0, last + 2 * NE)):
                pe.wait_ge(z_kept, kept)
                for m in range(M1 // P):
                    i = nc.tensor.matmul(ps[m][:, 0:P], t1[:, s, m * P:(m + 1) * P], Z[:, s, :],
                                         start=(s == 1), stop=(s == 0))
                    if s == 0:
                        i.then_inc(h1_done, 1)
            for s in range(M1 // P):
                pe.wait_ge(h1_kept_act, s + 1)
                for m in range(M2 // P):
                    i = nc.tensor.matmul(ps[6 + m][:, 0:P], t2[:, s, m * P:(m + 1) * P], h1[:, s, :],
                                         start=(s == 0), stop=(s == M1 // P - 1))
                    if s == M1 // P - 1:
                        i.then_inc(h2_done, 1)
            for s in range(M2 // P):
                pe.wait_ge(h2_kept, TILES + s)
                i = nc.tensor.matmul(psZ[1][0:1, 0:P], t3[:, s:s + 1], h2[:, s, :], start=(s == 0), stop=(s == M2 // P - 1))
            i.then_inc(y_done, 1)


def kernel(**inputs):
    import numpy as np
    import concourse.bacc as bacc
    from concourse.bass_utils import run_bass_kernel_spmd

    a = {k: np.asarray(v) for k, v in inputs.items()}
    w1, b1 = a["L0_rec_W1"], a["L0_rec_b1"]
    padded = np.zeros((H, NF, NF), w1.dtype)
    padded[:, :F, :F] = w1
    padded[:, F, F] = b1
    x, y = np.array(pair_columns()).T
    arrays = {
        "ids": np.ascontiguousarray(a["ids"]),
        "w1_xy": np.ascontiguousarray(padded[:, x, y]),
        "w1_yx": np.ascontiguousarray(padded[:, y, x]),
        "w2": np.ascontiguousarray(a["L0_rec_W2"].transpose(1, 2, 0)),
        "b2": np.ascontiguousarray(a["L0_rec_b2"].reshape(H, 1)),
        "dense": np.ascontiguousarray(a["dense_ctx"].T),
        "wt1": np.ascontiguousarray(a["W_top1"]),
        "bt1": np.ascontiguousarray(a["b_top1"].reshape(M1 // P, P).T),
        "wt2": np.ascontiguousarray(a["W_top2"]),
        "bt2": np.ascontiguousarray(a["b_top2"].reshape(M2 // P, P).T),
        "wt3": np.ascontiguousarray(a["W_top3"].reshape(M2 // P, P).T),
        "ident": np.eye(P, dtype=np.float32),
    }
    arrays["ids_looked"] = np.ascontiguousarray(a["ids"][:, LOOKED[0]:LOOKED[0] + NL].T)
    arrays["row_of"] = np.arange(VP * VS, dtype=np.float32).reshape(VP, VS)
    for f in range(F):
        arrays[f"tbl_{f}"] = np.ascontiguousarray(a[f"tbl_{f}"])
    nc = bacc.Bacc("TRN2", target_bir_lowering=False, num_devices=1)
    ap = {n: nc.dram_tensor(n, v.shape, mybir.dt.from_np(v.dtype), kind="ExternalInput").ap() for n, v in arrays.items()}
    out = nc.dram_tensor("y", (1, B), mybir.dt.float32, kind="ExternalOutput").ap()
    build(nc, ap["ids"], [ap[f"tbl_{f}"] for f in range(F)], ap["ids_looked"], ap["row_of"],
          ap["w1_xy"], ap["w1_yx"], ap["w2"], ap["b2"],
          ap["dense"], ap["wt1"], ap["bt1"], ap["wt2"], ap["bt2"], ap["wt3"], ap["ident"], out)
    r = run_bass_kernel_spmd(nc, [arrays], core_ids=[0])
    return r.results[0]["y"].reshape(B, 1)
```
